# Optimizing a Trainium2 kernel written in Bass

```python
import numpy as np
import jax
import jax.numpy as jnp

def _softmax(x, axis=-1):
    return jax.nn.softmax(x, axis=axis)

def _gelu(x):
    return jax.nn.gelu(x, approximate=True)

def _silu(x):
    return jax.nn.silu(x)

def _sigmoid(x):
    return jax.nn.sigmoid(x)

def _layernorm(x, axis=-1, eps=1e-05):
    m = jnp.mean(x, axis=axis, keepdims=True)
    v = jnp.var(x, axis=axis, keepdims=True)
    return (x - m) / jnp.sqrt(v + eps)

def _scatter_add(tgt, idx, src, axis=0):
    return tgt.at[idx].add(src)

def _segment_sum(src, seg, n):
    return jax.ops.segment_sum(src, seg, n)
kernel_name = 'mk_adj_ffn_d1_adj_r2_26b363'

def setup_inputs(seed: int=0):
    np.random.seed(seed)
    _w = jnp.asarray

    def _rec_inputs():
        import jax
        import jax.numpy as jnp
        _gk = jax.random.key(seed)
        x = -0.0005207 + 1.001 * jax.random.normal(jax.random.fold_in(_gk, 1), (32, 256, 256), jnp.float32)
        _a = jax.random.bernoulli(jax.random.fold_in(_gk, 2), 0.015625, (32, 256, 256))
        adj = _a.astype(jnp.int32)
        return (x, adj)
    x, adj = _rec_inputs()

    def _L0_gnn_setup():
        import jax, jax.numpy as jnp
        import numpy as np
        NEG_INF = -1e+30
        NEG_SLOPE = 0.2
        key = jax.random.key(seed)
        k1, k2, k3, k4, k5 = jax.random.split(key, 5)
        B, N, D, H = (2, 1024, 256, 8)
        k = D // H
        return {'x': jax.random.normal(k1, (B, N, D), dtype=jnp.float32), 'A': jax.random.randint(k2, (B, N, N), 0, 2, dtype=jnp.int32), 'W_proj': jax.random.normal(k3, (D, D), dtype=jnp.float32) * (1.0 / np.sqrt(D)), 'W_att': jax.random.normal(k4, (H, 2 * k), dtype=jnp.float32) * (1.0 / np.sqrt(2 * k)), 'b_att': jax.random.normal(k5, (H,), dtype=jnp.float32) * 0.01}
    _L0_gnn_all = _L0_gnn_setup()
    _L0_gnn_in = {k: v for k, v in _L0_gnn_all.items() if k in ('W_proj', 'W_att', 'b_att')}
    del _L0_gnn_all

    def _L0_ffn_setup():
        import jax, jax.numpy as jnp
        import numpy as np
        B, C, IN_LEN, OUT_LEN, E, TOP_K, N_I = (1, 4096, 256, 256, 8, 2, 16)
        key = jax.random.key(seed)
        ks = jax.random.split(key, 8)
        w = lambda k, shape, sc=0.02: jax.random.normal(k, shape, dtype=jnp.float32) * sc
        return {'x': jax.random.normal(ks[0], (B, C, IN_LEN), dtype=jnp.float32), 'Ins_tk': jax.random.normal(ks[1], (B, N_I, OUT_LEN), dtype=jnp.float32), 'gate_w': w(ks[2], (IN_LEN, E)), 'expert_w': w(ks[3], (E, IN_LEN, OUT_LEN)), 'expert_b': jnp.zeros((E, OUT_LEN), dtype=jnp.float32), 'gamma_w': w(ks[4], (E, OUT_LEN)), 'beta_w': w(ks[5], (E, OUT_LEN, OUT_LEN)), 'rmod_w': w(ks[6], (OUT_LEN, E))}
    _L0_ffn_all = _L0_ffn_setup()
    _L0_ffn_in = {k: v for k, v in _L0_ffn_all.items() if k in ('Ins_tk', 'gate_w', 'expert_w', 'expert_b', 'gamma_w', 'beta_w', 'rmod_w')}
    del _L0_ffn_all
    return {'x': x, 'adj': adj, 'L0_gnn_W_proj': _L0_gnn_in['W_proj'], 'L0_gnn_W_att': _L0_gnn_in['W_att'], 'L0_gnn_b_att': _L0_gnn_in['b_att'], 'L0_ffn_Ins_tk': _L0_ffn_in['Ins_tk'], 'L0_ffn_gate_w': _L0_ffn_in['gate_w'], 'L0_ffn_expert_w': _L0_ffn_in['expert_w'], 'L0_ffn_expert_b': _L0_ffn_in['expert_b'], 'L0_ffn_gamma_w': _L0_ffn_in['gamma_w'], 'L0_ffn_beta_w': _L0_ffn_in['beta_w'], 'L0_ffn_rmod_w': _L0_ffn_in['rmod_w']}

def reference(x, adj, L0_gnn_W_proj, L0_gnn_W_att, L0_gnn_b_att, L0_ffn_Ins_tk, L0_ffn_gate_w, L0_ffn_expert_w, L0_ffn_expert_b, L0_ffn_gamma_w, L0_ffn_beta_w, L0_ffn_rmod_w):
    import jax
    import jax.numpy as jnp

    def _L0_gnn_ref(x, A, W_proj, W_att, b_att):
        import jax, jax.numpy as jnp
        import numpy as np
        NEG_INF = -1e+30
        NEG_SLOPE = 0.2
        B, N, _ = x.shape
        H, two_k = W_att.shape
        k = two_k // 2
        xp = jnp.einsum('bnd,do->bno', x, W_proj)
        xh = xp.reshape(B, N, H, k).transpose(0, 2, 1, 3)
        a_src = jnp.einsum('bhnk,hk->bhn', xh, W_att[:, :k])
        a_dst = jnp.einsum('bhnk,hk->bhn', xh, W_att[:, k:])
        scores = a_src[:, :, :, None] + a_dst[:, :, None, :] + b_att[None, :, None, None]
        scores = jax.nn.leaky_relu(scores, negative_slope=NEG_SLOPE)
        mask = (A > 0)[:, None, :, :]
        scores = jnp.where(mask, scores, NEG_INF)
        att = jax.nn.softmax(scores, axis=-1)
        out = jax.nn.relu(jnp.einsum('bhij,bhjk->bhik', att, xh))
        return out.transpose(0, 2, 1, 3).reshape(B, N, H * k)

    def _L0_ffn_ref(x, Ins_tk, gate_w, expert_w, expert_b, gamma_w, beta_w, rmod_w):
        import jax, jax.numpy as jnp
        import numpy as np
        B, C, IN_LEN, OUT_LEN, E, TOP_K, N_I = (1, 4096, 256, 256, 8, 2, 16)
        Bx, Cx, L = x.shape
        xf = x.reshape(-1, L)
        ins = Ins_tk[0]
        router_gamma = jnp.mean(ins @ rmod_w, axis=0)
        logits = xf @ gate_w + router_gamma
        probs = jax.nn.softmax(logits.astype(jnp.float32), axis=-1)
        rw, sel = jax.lax.top_k(probs, TOP_K)
        combine = jnp.sum(jax.nn.one_hot(sel, E, dtype=rw.dtype) * rw[..., None], axis=1)
        gam = jnp.mean(ins @ gamma_w.T, axis=0)
        bet = jnp.einsum('nh,ehd->ed', ins, beta_w) / N_I
        eo = jnp.einsum('nl,eld->end', xf, expert_w) + expert_b[:, None, :]
        mod = gam[:, None, None] * eo + bet[:, None, :]
        out = jnp.einsum('ne,end->nd', combine, mod)
        return out.reshape(Bx, Cx, OUT_LEN)
    x = x + _L0_gnn_ref(_layernorm(x, axis=-1), adj, L0_gnn_W_proj, L0_gnn_W_att, L0_gnn_b_att)
    x = x + _L0_ffn_ref(_layernorm(x, axis=-1), L0_ffn_Ins_tk, L0_ffn_gate_w, L0_ffn_expert_w, L0_ffn_expert_b, L0_ffn_gamma_w, L0_ffn_beta_w, L0_ffn_rmod_w)
    return x

_drawn_inputs = setup_inputs


def setup_inputs(seed=0):
    import zlib

    import numpy as np

    out = dict(_drawn_inputs(seed))
    spreads = {'L0_ffn_expert_b': (0.0, 0.8)}
    factors = {'L0_gnn_b_att': 22.269,
     'L0_ffn_Ins_tk': 2.781,
     'L0_ffn_gate_w': 3.451,
     'L0_ffn_expert_w': 8.0,
     'L0_ffn_gamma_w': 8.0,
     'L0_ffn_beta_w': 2.882,
     'L0_ffn_rmod_w': 6.505}
    for name, (base, spread) in spreads.items():
        noise = np.random.default_rng([zlib.crc32(name.encode()), seed]).standard_normal(out[name].shape)
        drawn = base * np.exp(spread * noise) if base else spread * noise
        out[name] = jnp.asarray(drawn.astype(out[name].dtype))
    for name, factor in factors.items():
        out[name] = (out[name] * factor).astype(out[name].dtype)
    return out
```

```python
from contextlib import ExitStack

import concourse.bass as bass
from concourse import mybir

F32 = mybir.dt.float32
F32R = mybir.dt.float32r
BF16 = mybir.dt.bfloat16
I32 = mybir.dt.int32
ALU = mybir.AluOpType
ACT = mybir.ActivationFunctionType
AX = mybir.AxisListType

P = 128
EPS = 1e-5
SLOPE = 0.2
MASKED = -1e30
AR = 4
SENTINEL = -3e38


def program(nc, x, adj, W_proj, W_att, b_att, ins_tk, gate_w, expert_w, expert_b, gamma_t, beta_w, rmod_w, out):
    G, N, D = x.shape
    H, two_k = W_att.shape
    KH = two_k // 2
    E = gate_w.shape[1]
    NI = ins_tk.shape[1]
    T = N // P
    K = D // P
    HA = 2 * H
    assert T == 2 and K == 2 and H * KH == D and D == 256

    with ExitStack() as ctx:
        def sb(name, shape, dt=F32):
            return ctx.enter_context(nc.sbuf_tensor(name, shape, dt))

        def bank(name, dt=F32):
            return ctx.enter_context(nc.psum_tensor(name, [P, 512], dt))

        def sem(name):
            return ctx.enter_context(nc.semaphore(name))

        x_all = sb("x_all", [P, G, T, D])
        adj_ring = sb("adj_ring", [P, AR, T, N], I32)

        ident = sb("ident", [P, P])
        ones = sb("ones", [P, P])
        Wp = sb("Wp", [P, K, D + HA])
        Wph = sb("Wph", [P, K, D + HA], F32R)
        Wpl = sb("Wpl", [P, K, D + HA], F32R)
        Watt = sb("Watt", [P, H, 2, KH])
        batt = sb("batt", [P, H])
        wprod = sb("wprod", [P, H, KH])
        stage = sb("stage", [P, K, E, D])
        Weh = sb("Weh", [P, K, E, D], F32R)
        Wel = sb("Wel", [P, K, E, D], F32R)
        gate = sb("gate", [P, K, E])
        gateh = sb("gateh", [P, K, E], F32R)
        gatel = sb("gatel", [P, K, E], F32R)
        rmod = sb("rmod", [P, K, E])
        gammaT = sb("gammaT", [P, K, E])
        insr = sb("insr", [NI, D])
        ninv = sb("ninv", [NI, 1])
        insm = sb("insm", [P, K])
        gam_all = sb("gam_all", [P, E])
        gam_col = sb("gam_col", [E, 1])
        rgam = sb("rgam", [P, E])
        expb = sb("expb", [E, D])
        V = sb("V", [E, D])
        eye = sb("eye", [P, E, E])
        insd = sb("insd", [P, K, E, E])
        gamd = sb("gamd", [E, E])

        stats = sb("stats", [P, T, 6])
        mv = sb("mv", [P, T, 2])
        vare = sb("vare", [P, T])
        mhalf = sb("mhalf", [P, T])
        rstd = sb("rstd", [P, T])
        xn = sb("xn", [P, T, D])
        xTh = sb("xTh", [P, K, T, P], F32R)
        xTl = sb("xTl", [P, K, T, P], F32R)
        xh = sb("xh", [P, T, D])
        asrc = sb("asrc", [P, T, H])
        adst = sb("adst", [P, T, H])
        mbias = sb("mbias", [P, T, N])
        vsc = sb("vsc", [P, N])
        lsc = sb("lsc", [P, N])
        rmax = sb("rmax", [P, 4])
        prob = sb("prob", [P, N])
        psum_row = sb("psum_row", [P, 1])
        rrow = sb("rrow", [P, 1])
        probT = sb("probT", [P, T, P])
        att = sb("att", [P, T, D])

        lg = sb("lg", [P, T, 16])
        rep = sb("rep", [P, T, 16])
        m8 = sb("m8", [P, T, 8])
        vals = sb("vals", [P, T, 8])
        nmx = sb("nmx", [P, T])
        sel = sb("sel", [P, T, E])
        ex = sb("ex", [P, T, E])
        exs = sb("exs", [P, T])
        rex = sb("rex", [P, T])
        cmb = sb("cmb", [P, T, E])
        cT = sb("cT", [E, T, P])
        acc = sb("acc", [P, T, D])

        pT, pA, pB, pC = bank("pT"), bank("pA"), bank("pB"), bank("pC")
        pE = [bank(f"pE{i}") for i in range(4)]

        names = """diag id_zero id_one consts w_in att_in small_in exp_in beta_in watt_prod watt_sum wp_full wp_hi wp_lo
            insm_mm insm_sb mod_mm mod_sb gate_hi gate_lo exp_scaled exp_hi exp_lo bet_mm v_scaled v_sb gamc_mm gamc_sb
            x_in adj_in stats_d mv_d vare_d rstd_d xn_d xT_mm xTh_d xTl_d xp_mm xh_d asrc_d adst_d mask1 mask2
            bc_mm vmax_d top1 top2 top3 t_d l_d prob_d pT_mm pT_d o_mm rrow_d att_d x1_d
            fstats_d fmv_d fvare_d frstd_d fxn_d fxT_mm fxTh_d fxTl_d lg_mm lg_d m8_d vals_d rep_d sel_d nmx_d ex_d
            rex_d cmb_d cT_mm cT_d v_mm base_d e_mm e_acc out_d"""
        s = {n: sem(n) for n in names.split()}

        block = ctx.enter_context(nc.Block())

        @block.sync
        def _(sp):
            sp.sem_inc(s["out_d"], 16)
            sp.dma_start(Wp[:, :, 0:D], W_proj.rearrange("(k p) o -> p k o", p=P)).then_inc(s["w_in"], 16)
            sp.dma_start(Watt[:, :, :, :].rearrange("p h c k -> p (h c k)"),
                         W_att.rearrange("h k -> (h k)").partition_broadcast(P)).then_inc(s["att_in"], 16)
            sp.dma_start(batt[:, :], b_att.partition_broadcast(P)).then_inc(s["att_in"], 16)
            sp.dma_start(insr[:, :], ins_tk[0]).then_inc(s["small_in"], 16)
            sp.dma_start(gate[:, :, :], gate_w.rearrange("(k p) e -> p k e", p=P)).then_inc(s["small_in"], 16)
            sp.dma_start(rmod[:, :, :], rmod_w.rearrange("(k p) e -> p k e", p=P)).then_inc(s["small_in"], 16)
            sp.dma_start(gammaT[:, :, :], gamma_t.rearrange("(k p) e -> p k e", p=P)).then_inc(s["small_in"], 16)
            sp.dma_start(expb[:, :], expert_b).then_inc(s["small_in"], 16)
            sp.dma_start(x_all[:, 0], x[0].rearrange("(p t) d -> p t d", t=T)).then_inc(s["x_in"], 16)
            sp.dma_start(adj_ring[:, 0], adj[0].rearrange("(p t) n -> p t n", t=T)).then_inc(s["adj_in"], 16)
            for k in range(K):
                sp.dma_start(stage[:, k], expert_w[:, k * P:(k + 1) * P].rearrange("e p d -> p e d")).then_inc(s["exp_in"], 16)
            for first, last in ((1, AR), (AR, G)):
              with sp.Fori(first, last) as g:
                sp.wait_ge(s["x_in"], g * 16)
                sp.dma_start(x_all[:, g], x[g].rearrange("(p t) d -> p t d", t=T)).then_inc(s["x_in"], 16)
                sp.wait_ge(s["w_in"], 16)
                sp.wait_ge(s["adj_in"], g * 16)
                if first == AR:
                    sp.wait_ge(s["mask1"], (g - AR + 1) * T)
                sp.dma_start(adj_ring[:, g % AR], adj[g].rearrange("(p t) n -> p t n", t=T)).then_inc(s["adj_in"], 16)
            sp.wait_ge(s["exp_lo"], 1)
            for k in range(K):
                sp.dma_start(stage[:, k], beta_w[:, k * P:(k + 1) * P].rearrange("e p d -> p e d")).then_inc(s["beta_in"], 16)
            with sp.Fori(0, G) as g:
                sp.wait_ge(s["e_acc"], (g + 1) * T * E)
                sp.dma_start(out[g].rearrange("(p t) d -> p t d", t=T), acc[:, :, :]).then_inc(s["out_d"], 16)
            sp.wait_ge(s["out_d"], (G + 1) * 16)

        @block.gpsimd
        def _(pool):
            pool.memset(ident[:, :], 0.0).then_inc(s["id_zero"], 1)
            pool.memset(ones[:, :], 1.0).then_inc(s["consts"], 1)
            pool.memset(mhalf[:, :], -0.5).then_inc(s["consts"], 1)
            pool.memset(ninv[:, :], 1.0 / NI).then_inc(s["consts"], 1)
            pool.memset(vals[:, :, :], SENTINEL).then_inc(s["consts"], 1)
            pool.memset(lg[:, :, :], SENTINEL).then_inc(s["consts"], 1)
            pool.memset(eye[:, :, :], 0.0).then_inc(s["id_zero"], 1)
            pool.wait_ge(s["id_zero"], 2)
            pool.affine_select(out=eye[:, :, :], in_=eye[:, :, :], compare_op=ALU.not_equal, fill=1.0, base=0,
                               pattern=[[1, E], [-1, E]], channel_multiplier=0).then_inc(s["id_one"], 1)
            pool.affine_select(out=ident[:, :], in_=ident[:, :], compare_op=ALU.not_equal, fill=1.0, base=0,
                               pattern=[[-1, P]], channel_multiplier=1).then_inc(s["id_one"], 1)
            with pool.Fori(0, G) as g:
                mv_done = pool.to_reg((g + 1) * T)
                pool.wait_ge(s["id_zero"], 2)
                pool.wait_ge(s["mv_d"], mv_done)
                pool.tensor_scalar(vare[:, :], mv[:, :, 1], EPS, None, ALU.add).then_inc(s["vare_d"], 1)
                pool.wait_ge(s["vare_d"], g + 1)
                pool.tensor_tensor(rstd[:, :], vare[:, :], mhalf[:, :], ALU.pow).then_inc(s["rstd_d"], 1)
            with pool.Fori(0, G) as g:
                mv_done = pool.to_reg((g + 1) * T)
                pool.wait_ge(s["id_zero"], 2)
                pool.wait_ge(s["fmv_d"], mv_done)
                pool.tensor_scalar(vare[:, :], mv[:, :, 1], EPS, None, ALU.add).then_inc(s["fvare_d"], 1)
                pool.wait_ge(s["fvare_d"], g + 1)
                pool.tensor_tensor(rstd[:, :], vare[:, :], mhalf[:, :], ALU.pow).then_inc(s["frstd_d"], 1)

        @block.scalar
        def _(act):
            with act.Fori(0, G) as g:
                act.wait_ge(s["xT_mm"], g + 1)
                act.activation(xTh[:, :, :, :].rearrange("p k t n -> p (k t n)"), pT[:, :], ACT.Copy).then_inc(s["xTh_d"], 1)
                act.wait_ge(s["xp_mm"], (g + 1))
                for t, bk in enumerate((pA, pB)):
                    act.activation(xh[:, t, :], bk[:, 0:D], ACT.Copy).then_inc(s["xh_d"], 1)
                for n in range(T * H):
                    act.wait_ge(s["l_d"], g * T * H + n + 1)
                    act.activation(prob[:, :], lsc[:, :], ACT.Exp, bias=rmax[:, 3:4], accum_out=psum_row[:, :]).then_inc(s["prob_d"], 1)
                    act.wait_ge(s["pT_mm"], g * T * H + n + 1)
                    act.activation(probT[:, :, :].rearrange("p t n -> p (t n)"), pT[:, 0:N], ACT.Copy).then_inc(s["pT_d"], 1)
            with act.Fori(0, G) as g:
                act.wait_ge(s["fxT_mm"], g + 1)
                act.activation(xTh[:, :, :, :].rearrange("p k t n -> p (k t n)"), pT[:, :], ACT.Copy).then_inc(s["fxTh_d"], 1)
                for t in range(T):
                    act.wait_ge(s["nmx_d"], g * T + t + 1)
                    act.activation(ex[:, t, :], lg[:, t, 0:E], ACT.Exp, bias=nmx[:, t:t + 1], accum_out=exs[:, t:t + 1]).then_inc(s["ex_d"], 1)
                act.wait_ge(s["cT_mm"], g + 1)
                act.activation(cT[:, :, :].rearrange("e t n -> e (t n)"), pB[0:E, 0:N], ACT.Copy).then_inc(s["cT_d"], 1)

        @block.vector
        def _(dve):
            dve.wait_ge(s["w_in"], 16)
            dve.wait_ge(s["att_in"], 32)
            n = 0
            for k in range(K):
                for c in range(2):
                    if n:
                        dve.wait_ge(s["watt_sum"], n)
                    dve.tensor_tensor(wprod[:, :, :], Wp[:, k, 0:D].rearrange("p (h k) -> p h k", h=H), Watt[:, :, c, :],
                                      ALU.mult).then_inc(s["watt_prod"], 1)
                    n += 1
                    dve.wait_ge(s["watt_prod"], n)
                    dve.tensor_reduce(Wp[:, k, D + c * H:D + (c + 1) * H], wprod[:, :, :], AX.X, ALU.add).then_inc(s["watt_sum"], 1)
            dve.wait_ge(s["watt_sum"], n)
            dve.tensor_copy(Wph[:, :, :], Wp[:, :, :]).then_inc(s["wp_hi"], 1)
            dve.wait_ge(s["wp_hi"], 1)
            dve.tensor_tensor(Wpl[:, :, :], Wp[:, :, :], Wph[:, :, :].bitcast(F32), ALU.subtract).then_inc(s["wp_lo"], 1)
            dve.wait_ge(s["small_in"], 16 * 5)
            dve.tensor_copy(gateh[:, :, :], gate[:, :, :]).then_inc(s["gate_hi"], 1)
            dve.wait_ge(s["gate_hi"], 1)
            dve.tensor_tensor(gatel[:, :, :], gate[:, :, :], gateh[:, :, :].bitcast(F32), ALU.subtract).then_inc(s["gate_lo"], 1)
            dve.wait_ge(s["insm_mm"], 1)
            dve.tensor_copy(insm[:, :], pC[:, 0:K]).then_inc(s["insm_sb"], 1)
            dve.wait_ge(s["mod_mm"], 1)
            dve.tensor_copy(gam_all[:, :], pC[:, 16:16 + E]).then_inc(s["mod_sb"], 1)
            dve.tensor_copy(rgam[:, :], pC[:, 32:32 + E]).then_inc(s["mod_sb"], 1)
            dve.tensor_copy(gam_col[:, :], pC[0:E, 48:49]).then_inc(s["mod_sb"], 1)
            dve.wait_ge(s["mod_sb"], 3)
            dve.wait_ge(s["id_one"], 2)
            for k in range(K):
                dve.tensor_scalar(insd[:, k], eye[:, :, :], insm[:, k:k + 1], None, ALU.mult).then_inc(s["diag"], 1)
            dve.tensor_scalar(gamd[:, :], ident[0:E, 0:E], gam_col[:, 0:1], None, ALU.mult).then_inc(s["diag"], 1)
            dve.wait_ge(s["exp_in"], 16 * K)
            for e in range(E):
                dve.tensor_scalar(stage[:, :, e, :], stage[:, :, e, :], gam_all[:, e:e + 1], None, ALU.mult).then_inc(s["exp_scaled"], 1)
            dve.wait_ge(s["exp_scaled"], E)
            dve.tensor_copy(Weh[:, :, :, :], stage[:, :, :, :]).then_inc(s["exp_hi"], 1)
            dve.wait_ge(s["exp_hi"], 1)
            dve.tensor_tensor(Wel[:, :, :, :], stage[:, :, :, :], Weh[:, :, :, :].bitcast(F32), ALU.subtract).then_inc(s["exp_lo"], 1)

            with dve.Fori(0, G) as g:
                dve.wait_ge(s["x_in"], (g + 1) * 16)
                for t in range(T):
                    dve.bn_stats(stats[:, t, :], x_all[:, g, t, :]).then_inc(s["stats_d"], 1)
                for t in range(T):
                    stats_done = dve.to_reg(g * T + t + 1)
                    dve.wait_ge(s["id_one"], 2)
                    dve.wait_ge(s["stats_d"], stats_done)
                    dve.bn_aggr(mv[:, t, :], stats[:, t, :]).then_inc(s["mv_d"], 1)
                dve.wait_ge(s["rstd_d"], g + 1)
                for t in range(T):
                    dve.tensor_scalar(xn[:, t, :], x_all[:, g, t, :], mv[:, t, 0:1], rstd[:, t:t + 1], ALU.subtract,
                                      ALU.mult).then_inc(s["xn_d"], 1)
                dve.wait_ge(s["xTh_d"], g + 1)
                dve.tensor_tensor(xTl[:, :, :, :].rearrange("p k t n -> p (k t n)"), pT[:, :],
                                  xTh[:, :, :, :].rearrange("p k t n -> p (k t n)").bitcast(F32), ALU.subtract).then_inc(s["xTl_d"], 1)
                dve.wait_ge(s["xh_d"], (g + 1) * T)
                for t, bk in enumerate((pA, pB)):
                    dve.tensor_tensor(asrc[:, t, :], bk[:, D:D + H], batt[:, :], ALU.add).then_inc(s["asrc_d"], 1)
                    dve.tensor_copy(adst[:, t, :], bk[:, D + H:D + HA]).then_inc(s["adst_d"], 1)
                dve.wait_ge(s["adj_in"], (g + 1) * 16)
                for t in range(T):
                    dve.tensor_scalar(mbias[:, t, :].rearrange("p (u q) -> p u q", u=T),
                                      adj_ring[:, g % AR, t, :].rearrange("p (q u) -> p u q", u=T), 0, None, ALU.is_gt).then_inc(s["mask1"], 1)
                dve.wait_ge(s["mask1"], (g + 1) * T)
                dve.tensor_scalar(mbias[:, :, :], mbias[:, :, :], -MASKED, MASKED, ALU.mult, ALU.add).then_inc(s["mask2"], 1)
                dve.wait_ge(s["mask2"], g + 1)
                dve.wait_ge(s["asrc_d"], (g + 1) * T)
                for n in range(T * H):
                    t, h = n // H, n % H
                    i = dve.to_reg(g * T * H + n + 1)
                    dve.wait_ge(s["id_one"], 2)
                    dve.wait_ge(s["bc_mm"], i)
                    dve.tensor_tensor_reduce(vsc[:, :], pC[:, 0:N], mbias[:, t, :], 1.0, -3e38, ALU.add, ALU.max,
                                             rmax[:, 0:1]).then_inc(s["vmax_d"], 1)
                    dve.wait_ge(s["vmax_d"], i)
                    dve.tensor_scalar(rmax[:, 1:2], rmax[:, 0:1], asrc[:, t, h:h + 1], None, ALU.add).then_inc(s["top1"], 1)
                    dve.tensor_scalar(vsc[:, :], vsc[:, :], asrc[:, t, h:h + 1], None, ALU.add).then_inc(s["t_d"], 1)
                    dve.wait_ge(s["top1"], i)
                    dve.scalar_tensor_tensor(rmax[:, 2:3], rmax[:, 1:2], SLOPE, rmax[:, 1:2], ALU.mult, ALU.max).then_inc(s["top2"], 1)
                    dve.wait_ge(s["t_d"], i)
                    dve.scalar_tensor_tensor(lsc[:, :], vsc[:, :], SLOPE, vsc[:, :], ALU.mult, ALU.max)
                    dve.wait_ge(s["top2"], i)
                    dve.tensor_scalar(rmax[:, 3:4], rmax[:, 2:3], -1.0, None, ALU.mult).then_inc(s["l_d"], 1)
                    dve.wait_ge(s["prob_d"], i)
                    dve.reciprocal(rrow[:, :], psum_row[:, :]).then_inc(s["rrow_d"], 1)
                    dve.wait_ge(s["rrow_d"], i)
                    dve.wait_ge(s["o_mm"], i)
                    dve.tensor_scalar(att[:, t, h * KH:(h + 1) * KH], pA[:, 0:KH], rrow[:, :], None, ALU.mult).then_inc(s["att_d"], 1)
                dve.wait_ge(s["att_d"], (g + 1) * T * H)
                dve.scalar_tensor_tensor(x_all[:, g], att[:, :, :], 0.0, x_all[:, g], ALU.max, ALU.add).then_inc(s["x1_d"], 1)

            dve.wait_ge(s["bet_mm"], 1)
            dve.tensor_copy(V[:, :], pC[0:E, 0:D]).then_inc(s["v_sb"], 1)
            with dve.Fori(0, G) as g:
                dve.wait_ge(s["x1_d"], g + 1)
                for t in range(T):
                    dve.bn_stats(stats[:, t, :], x_all[:, g, t, :]).then_inc(s["fstats_d"], 1)
                for t in range(T):
                    stats_done = dve.to_reg(g * T + t + 1)
                    dve.wait_ge(s["id_one"], 2)
                    dve.wait_ge(s["fstats_d"], stats_done)
                    dve.bn_aggr(mv[:, t, :], stats[:, t, :]).then_inc(s["fmv_d"], 1)
                dve.wait_ge(s["frstd_d"], g + 1)
                for t in range(T):
                    dve.tensor_scalar(xn[:, t, :], x_all[:, g, t, :], mv[:, t, 0:1], rstd[:, t:t + 1], ALU.subtract,
                                      ALU.mult).then_inc(s["fxn_d"], 1)
                dve.wait_ge(s["fxTh_d"], g + 1)
                dve.tensor_tensor(xTl[:, :, :, :].rearrange("p k t n -> p (k t n)"), pT[:, :],
                                  xTh[:, :, :, :].rearrange("p k t n -> p (k t n)").bitcast(F32), ALU.subtract).then_inc(s["fxTl_d"], 1)
                dve.wait_ge(s["lg_mm"], g + 1)
                dve.wait_ge(s["consts"], 5)
                for t in range(T):
                    dve.tensor_tensor(lg[:, t, 0:E], pA[:, t * E:(t + 1) * E], rgam[:, :], ALU.add).then_inc(s["lg_d"], 1)
                for t in range(T):
                    i = dve.snap(g * T + t + 1)
                    dve.wait_ge(s["id_one"], 2)
                    dve.wait_ge(s["lg_d"], i)
                    dve.max(m8[:, t, :], lg[:, t, 0:E]).then_inc(s["m8_d"], 1)
                    dve.wait_ge(s["m8_d"], i)
                    dve.tensor_scalar(nmx[:, t:t + 1], m8[:, t, 0:1], -1.0, None, ALU.mult).then_inc(s["nmx_d"], 1)
                    dve.tensor_copy(vals[:, t, 0:2], m8[:, t, 0:2]).then_inc(s["vals_d"], 1)
                    dve.wait_ge(s["id_one"], 2)
                    dve.wait_ge(s["vals_d"], i)
                    dve.match_replace(rep[:, t, 0:14], vals[:, t, :], lg[:, t, 0:14], SENTINEL).then_inc(s["rep_d"], 1)
                    dve.wait_ge(s["rep_d"], i)
                    dve.tensor_tensor(sel[:, t, :], rep[:, t, 0:E], lg[:, t, 0:E], ALU.not_equal).then_inc(s["sel_d"], 1)
                    dve.wait_ge(s["ex_d"], i)
                    dve.reciprocal(rex[:, t:t + 1], exs[:, t:t + 1]).then_inc(s["rex_d"], 1)
                    dve.wait_ge(s["rex_d"], i)
                    dve.wait_ge(s["sel_d"], i)
                    dve.scalar_tensor_tensor(cmb[:, t, :], ex[:, t, :], rex[:, t:t + 1], sel[:, t, :], ALU.mult, ALU.mult).then_inc(s["cmb_d"], 1)
                dve.wait_ge(s["v_mm"], g + 1)
                dve.wait_ge(s["out_d"], (g + 1) * 16)
                dve.tensor_tensor(acc[:, :, :], pC[:, :].rearrange("p (t d) -> p t d", t=T), x_all[:, g], ALU.add).then_inc(s["base_d"], 1)
                dve.wait_ge(s["base_d"], g + 1)
                dve.wait_ge(s["cmb_d"], (g + 1) * T)
                for n in range(T * E):
                    e, t = n // (2 * T) * 2 + n % 2, n // 2 % T
                    b = n // 2
                    dve.wait_ge(s["e_mm"], g * T * E // 2 + b + 1)
                    if n:
                        dve.wait_ge(s["e_acc"], g * T * E + n)
                    dve.scalar_tensor_tensor(acc[:, t, :], pE[b % 4][:, (n % 2) * D:(n % 2 + 1) * D], cmb[:, t, e:e + 1],
                                             acc[:, t, :], ALU.mult, ALU.add).then_inc(s["e_acc"], 1)

        @block.tensor
        def _(pe):
            pe.wait_ge(s["consts"], 5)
            pe.wait_ge(s["id_one"], 2)
            pe.wait_ge(s["small_in"], 16 * 5)
            for k in range(K):
                mm = pe.matmul(pC[:, k:k + 1], insr[:, k * P:(k + 1) * P], ninv[:, :], start=True, stop=True)
            mm.then_inc(s["insm_mm"], 1)
            pe.wait_ge(s["insm_sb"], 1)
            for k in range(K):
                pe.matmul(pC[:, 16:16 + E], insm[:, k:k + 1].broadcast_to([P, P]), gammaT[:, k, :], start=k == 0, stop=k == K - 1)
            for k in range(K):
                pe.matmul(pC[:, 32:32 + E], insm[:, k:k + 1].broadcast_to([P, P]), rmod[:, k, :], start=k == 0, stop=k == K - 1)
            for k in range(K):
                mm = pe.matmul(pC[0:E, 48:49], gammaT[:, k, :], insm[:, k:k + 1], start=k == 0, stop=k == K - 1)
            mm.then_inc(s["mod_mm"], 1)
            pe.wait_ge(s["wp_lo"], 1)
            with pe.Fori(0, G) as g:
                pe.wait_ge(s["xn_d"], (g + 1) * T)
                for k in range(K):
                    for t in range(T):
                        mm = pe.transpose(pT[:, (k * T + t) * P:(k * T + t + 1) * P], xn[:, t, k * P:(k + 1) * P], ident[:, :])
                mm.then_inc(s["xT_mm"], 1)
                pe.wait_ge(s["xTl_d"], g + 1)
                for t, bk in enumerate((pA, pB)):
                    for k in range(K):
                        for i, (a, b) in enumerate(((xTh, Wph), (xTh, Wpl), (xTl, Wph))):
                            mm = pe.matmul(bk[:, 0:D + HA], a[:, k, t, :], b[:, k, :], start=k == 0 and i == 0, stop=k == K - 1 and i == 2)
                mm.then_inc(s["xp_mm"], 1)
                pe.wait_ge(s["adst_d"], (g + 1) * T)
                pe.wait_ge(s["xh_d"], (g + 1) * T)
                for n in range(T * H):
                    t, h = n // H, n % H
                    i = g * T * H + n + 1
                    if n:
                        pe.wait_ge(s["vmax_d"], i - 1)
                    for u in range(T):
                        mm = pe.transpose(pC[:, u * P:(u + 1) * P], adst[:, u, h:h + 1].broadcast_to([P, P]), ident[:, :])
                    mm.then_inc(s["bc_mm"], 1)
                    pe.wait_ge(s["prob_d"], i)
                    for u in range(T):
                        mm = pe.transpose(pT[:, u * P:(u + 1) * P], prob[:, u * P:(u + 1) * P], ident[:, :])
                    mm.then_inc(s["pT_mm"], 1)
                    pe.wait_ge(s["pT_d"], i)
                    if n:
                        pe.wait_ge(s["att_d"], i - 1)
                    for u in range(T):
                        mm = pe.matmul(pA[:, 0:KH], probT[:, u, :], xh[:, u, h * KH:(h + 1) * KH], start=u == 0, stop=u == T - 1)
                    mm.then_inc(s["o_mm"], 1)
            pe.wait_ge(s["beta_in"], 16 * K)
            pe.wait_ge(s["diag"], K + 1)
            pe.wait_ge(s["x1_d"], G)
            for e in range(E):
                for k in range(K):
                    pe.matmul(pC[0:E, 0:D], insd[:, k, e, :], stage[:, k, e, :], start=e + k == 0, stop=False)
            pe.matmul(pC[0:E, 0:D], gamd[:, :], expb[:, :], start=False, stop=True).then_inc(s["bet_mm"], 1)
            pe.wait_ge(s["v_sb"], 1)
            with pe.Fori(0, G) as g:
                pe.wait_ge(s["fxn_d"], (g + 1) * T)
                for k in range(K):
                    for t in range(T):
                        mm = pe.transpose(pT[:, (k * T + t) * P:(k * T + t + 1) * P], xn[:, t, k * P:(k + 1) * P], ident[:, :])
                mm.then_inc(s["fxT_mm"], 1)
                pe.wait_ge(s["fxTl_d"], g + 1)
                for t in range(T):
                    for k in range(K):
                        for i, (a, b) in enumerate(((xTh, gateh), (xTh, gatel), (xTl, gateh))):
                            mm = pe.matmul(pA[:, t * E:(t + 1) * E], a[:, k, t, :], b[:, k, :], start=k == 0 and i == 0, stop=k == K - 1 and i == 2)
                mm.then_inc(s["lg_mm"], 1)
                pe.wait_ge(s["cmb_d"], (g + 1) * T)
                for t in range(T):
                    mm = pe.transpose(pB[0:E, t * P:(t + 1) * P], cmb[:, t, :], ident[:, :])
                mm.then_inc(s["cT_mm"], 1)
                pe.wait_ge(s["cT_d"], g + 1)
                for t in range(T):
                    mm = pe.matmul(pC[:, t * D:(t + 1) * D], cT[:, t, :], V[:, :], start=True, stop=True)
                mm.then_inc(s["v_mm"], 1)
                for b in range(T * E // 2):
                    q, t = b // T, b % T
                    if b >= 4:
                        pe.wait_ge(s["e_acc"], g * T * E + 2 * (b - 3))
                    for k in range(K):
                        for i, (a, w) in enumerate(((xTh, Weh), (xTh, Wel), (xTl, Weh))):
                            mm = pe.matmul(pE[b % 4][:, :], a[:, k, t, :], w[:, k, 2 * q:2 * q + 2, :].rearrange("p e d -> p (e d)"),
                                           start=k == 0 and i == 0, stop=k == K - 1 and i == 2)
                    mm.then_inc(s["e_mm"], 1)



_INS = ["x", "adj", "L0_gnn_W_proj", "L0_gnn_W_att", "L0_gnn_b_att", "L0_ffn_Ins_tk", "L0_ffn_gate_w",
        "L0_ffn_expert_w", "L0_ffn_expert_b", "L0_ffn_gamma_w", "L0_ffn_beta_w", "L0_ffn_rmod_w"]


def kernel(**inputs):
    import concourse.bacc as bacc
    import numpy as np
    from concourse.bass_utils import run_bass_kernel_spmd

    nc = bacc.Bacc("TRN2", target_bir_lowering=False, num_devices=1)
    arrays, args = {}, []
    for name in _INS:
        a = np.asarray(inputs[name])
        a = np.ascontiguousarray(a.T if name == "L0_ffn_gamma_w" else a)
        arrays[f"in_{name}"] = a
        args.append(nc.dram_tensor(f"in_{name}", a.shape, mybir.dt.from_np(a.dtype), kind="ExternalInput").ap())
    out = nc.dram_tensor("out", arrays["in_x"].shape, F32, kind="ExternalOutput").ap()
    program(nc, *args, out)
    result = run_bass_kernel_spmd(nc, [arrays], core_ids=[0])
    return result.results[0]["out"]
```

```python
from contextlib import ExitStack

import concourse.bass as bass
from concourse import mybir

F32 = mybir.dt.float32
F32R = mybir.dt.float32r
BF16 = mybir.dt.bfloat16
I32 = mybir.dt.int32
ALU = mybir.AluOpType
ACT = mybir.ActivationFunctionType
AX = mybir.AxisListType

P = 128
EPS = 1e-5
SLOPE = 0.2
MASKED = -1e30
SENTINEL = -3e38
BOUND = 30.0
AR = 2
RING = 8
PARTS = 3
LAG = 5


def program(nc, x, adj, W_proj, W_att, b_att, ins_tk, gate_w, expert_w, expert_b, gamma_t, beta_w, rmod_w, out):
    G, N, D = x.shape
    H, two_k = W_att.shape
    KH = two_k // 2
    E = gate_w.shape[1]
    NI = ins_tk.shape[1]
    T = N // P
    K = D // P
    HA = 2 * H
    X1 = KH + 1
    assert T == 2 and K == 2 and H * KH == D and D == N and E == 8 and G % 2 == 0

    row_dram = nc.dram_tensor("row_dram", [2, H * N], F32, kind="Internal").ap()

    with ExitStack() as ctx:
        def sb(name, shape, dt=F32):
            return ctx.enter_context(nc.sbuf_tensor(name, shape, dt))

        def bank(name, n=1):
            return ctx.enter_context(nc.psum_tensor(name, [P, 512] if n == 1 else [P, n, 512], F32))

        def sem(name):
            return ctx.enter_context(nc.semaphore(name))

        x_all = sb("x_all", [P, G, T, D])
        abc = x_all[:, RING:2 * RING].rearrange("p (b g) t d -> p b (g t d)", b=2)
        beta_sb = x_all[:, RING:2 * RING].rearrange("p (k g) t d -> p k (g t) d", k=K)
        ybuf = x_all[:, 2 * RING:2 * RING + 6]
        adj_ring = sb("adj_ring", [P, AR, T, N], I32)

        ident = sb("ident", [P, P])
        ident16 = sb("ident16", [P, P], BF16)
        ones = sb("ones", [P, P])
        mean_w = sb("mean_w", [P, P])
        Wp = sb("Wp", [P, K, D + HA])
        Wph = sb("Wph", [P, K, D + HA], F32R)
        Wpl = sb("Wpl", [P, K, D + HA], F32R)
        Watt = sb("Watt", [P, H, 2, KH])
        batt = sb("batt", [P, H])
        wprod = sb("wprod", [P, H, KH])
        wsq = sb("wsq", [P, K, HA])
        bnd = sb("bnd", [P, 6])
        flag = sb("flag", [P, 1], I32)
        big = sb("big", [P, K, E, D])
        Q = big[:, :, :, :].rearrange("p k e d -> p (k e d)").bitcast(BF16).rearrange("p (b u h i) -> p b u h i", b=2, u=T, h=H)
        Weh = sb("Weh", [P, K, E, D], F32R)
        Wel = sb("Wel", [P, K, E, D], F32R)
        gate = sb("gate", [P, K, E])
        gateh = sb("gateh", [P, K, E], F32R)
        gatel = sb("gatel", [P, K, E], F32R)
        rmod = sb("rmod", [P, K, E])
        gammaT = sb("gammaT", [P, K, E])
        insr = sb("insr", [NI, D])
        ninv = sb("ninv", [NI, 1])
        insm = sb("insm", [P, K])
        gam_all = sb("gam_all", [P, E])
        gam_col = sb("gam_col", [E, 1])
        rgam = sb("rgam", [P, E])
        expb = sb("expb", [E, D])
        eye = sb("eye", [P, E, E])
        insd = sb("insd", [P, K, E, 3, E])
        gamd = sb("gamd", [E, 3, E])
        Vr = sb("Vr", [3 * E, D])
        Vh = sb("Vh", [3 * E, D], F32R)
        Vl = sb("Vl", [3 * E, D])
        V3 = sb("V3", [3 * E, D], F32R)
        rowsel = sb("rowsel", [3 * E, 2])
        V = Vr[0:E, :]

        stats = sb("stats", [P, T, 6])
        mv = sb("mv", [P, T, 2])
        vare = sb("vare", [P, T])
        mhalf = sb("mhalf", [P, T])
        rstd = sb("rstd", [P, T])
        xn = sb("xn", [P, T, D])
        xTh = sb("xTh", [P, K, T, P], F32R)
        xTl = sb("xTl", [P, K, T, P], F32R)
        stats2 = sb("stats2", [P, T, 6])
        mv2 = sb("mv2", [P, T, 2])
        vare2 = sb("vare2", [P, T])
        rstd2 = sb("rstd2", [P, T])
        xf = sb("xf", [P, T, D])
        fTh = sb("fTh", [P, 2, K, T, P], F32R)
        fTl = sb("fTl", [P, 2, K, T, P], F32R)

        xh1 = sb("xh1", [P, 2, T, H, X1])
        ab = sb("ab", [P, T, HA])
        asrc2 = sb("asrc2", [P, 2, T, H])
        negb = sb("negb", [P, 2, T, H])
        beta2 = sb("beta2", [P, T, H, 2])
        rho = sb("rho", [P, 2, T, H])
        mb = sb("mb", [P, T, T, P], BF16)
        mtn = sb("mtn", [P, 2, T, N], BF16)
        mt = sb("mt", [P, 2, T, N], BF16)
        arow = sb("arow", [H, N])
        xe = sb("xe", [P, T, H, 2, X1])
        xp = sb("xp", [P, 2, T, PARTS, H * 2 * X1], BF16)
        sbc = sb("sbc", [P, 2, D])
        nt = sb("nt", [P, T, H, X1])
        nn = sb("nn", [P, T, H, X1])
        emp = sb("emp", [P, T, 1])
        dsum = sb("dsum", [P, T, H])
        rden = sb("rden", [P, T, H])
        oo = sb("oo", [P, T, D])

        spare = xp[:, :, :, :, :].rearrange("p b t c n -> p (b t c n)").bitcast(F32)
        mbias = spare[:, 0:512].rearrange("p (t n) -> p t n", t=T)
        att = spare[:, 512:1024].rearrange("p (t n) -> p t n", t=T)
        vsc, lsc, prob = (spare[:, 1024 + i * 256:1280 + i * 256] for i in range(3))
        probT = spare[:, 1792:2048].rearrange("p (t n) -> p t n", t=T)
        xh = xe[:, :, :, :, :].rearrange("p t h c k -> p (t h c k)")[:, 0:T * D].rearrange("p (t d) -> p t d", t=T)
        asrc, adst = asrc2[:, 0], asrc2[:, 1]
        rmax = sb("rmax", [P, 4])
        psum_row = sb("psum_row", [P, 1])
        rrow = sb("rrow", [P, 1])

        lgT = sb("lgT", [E, N])
        lg = sb("lg", [P, T, 16])
        rep = sb("rep", [P, T, 16])
        m8 = sb("m8", [P, T, 8])
        vals = sb("vals", [P, T, 8])
        nmx = sb("nmx", [P, T])
        lgm = sb("lgm", [P, T, E])
        sel = sb("sel", [P, T, E])
        ex = sb("ex", [P, T, E])
        exs = sb("exs", [P, T])
        rex = sb("rex", [P, T])
        exsel = sb("exsel", [P, T, E])
        cmb2 = sb("cmb2", [P, 2, T, E])
        cmb = cmb2[:, 0]
        c3 = sb("c3", [P, T, 3, E])
        cT = sb("cT", [E, T, P])
        cT3 = sb("cT3", [3 * E, 2, T, P], F32R)
        acc2 = sb("acc2", [P, 2, T, D])
        acc = acc2[:, 0]
        yfold = sb("yfold", [P, 2, T, D])

        bT, bX, bS = bank("bT"), bank("bX"), bank("bS")
        bR = bank("bR", 2)
        bE = [bank(f"bE{i}") for i in range(3)]
        pT, pA, pB, pC = bT, bX, bS, bR[:, 0]
        pE = [bR[:, 1], *bE]

        names = """id_zero id_one eye16 consts w_in att_in small_in exp_in beta_in watt_prod watt_sum wp_hi wp_lo
            insm_mm insm_sb mod_mm mod_sb diag gate_hi gate_lo exp_scaled exp_hi exp_lo bet_mm v_raw v_hi v_lo v_sel v_sb
            wsq_d wsq_mm bnd_max bnd_ok flag_d x_in adj_in"""
        fast_names = """a_stats a_mv a_var a_rstd a_xn a_xT a_hi a_lo a_xp a_ev a_src a_neg a_beta a_mb a_mT a_mneg a_rT a_row
            row_out abc_in b_q b_mt b_rho b_xe b_p0 b_r b_p1 b_p2 b_S b_Sb
            r_mm r_t0 r_n r_e r_ds r_rd r_o r_z r_x1
            c_stats c_mv c_var c_rstd c_xn c_xT c_hi c_lo c_lT c_lTs c_lb c_lg c_m8 c_vals c_lgm c_rep c_sel c_ex c_sum
            c_rec c_es c_cmb c_ch c_cl c_c3 c_cT c_cTs
            d_mm d_dve d_act d_link d_pool f_fin f_out"""
        slow_names = """stats_d mv_d vare_d rstd_d xn_d xT_mm xTh_d xTl_d xp_mm xh_d asrc_d adst_d mask1 mask2
            bc_mm vmax_d top1 top2 t_d l_d prob_d pT_mm pT_d o_mm rrow_d att_d x1_d
            fstats_d fmv_d fvare_d frstd_d fxn_d fxT_mm fxTh_d fxTl_d lg_mm lg_d m8_d vals_d rep_d sel_d nmx_d ex_d
            rex_d cmb_d cT_mm cT_d v_mm base_d e_mm e_acc out_d"""
        s = {n: sem(n) for n in (names + " " + fast_names).split()}
        s.update(zip(slow_names.split(), (s[n] for n in fast_names.split())))
        assert len(slow_names.split()) <= len(fast_names.split())

        def held(eng, name, value, const=("id_one", 2)):
            if isinstance(value, int):
                eng.wait_ge(s[name], value)
            else:
                register = eng.to_reg(value)
                eng.wait_ge(s[const[0]], const[1])
                eng.wait_ge(s[name], register)

        def fast_path(eng):
            eng.wait_ge(s["flag_d"], 1)
            return eng.value_load(flag[0:1, 0:1], min_val=0, max_val=1)

        def iterations(eng, body, end=G):
            def graphs(it):
                return [it - i if 0 <= it - i < G else None for i in range(LAG + 1)]

            for it in range(LAG + 1):
                body(it % 2, *graphs(it))
            with eng.Fori(LAG + 1, end, 2) as it:
                body(0, *(it - i for i in range(LAG + 1)))
                body(1, *(it + 1 - i for i in range(LAG + 1)))
            for it in range(end, G + LAG):
                body(it % 2, *graphs(it))

        block = ctx.enter_context(nc.Block())

        @block.sync
        def _(sp):
            def load_x(g, slot):
                sp.dma_start(x_all[:, slot], x[g].rearrange("(p t) d -> p t d", t=T)).then_inc(s["x_in"], 16)

            def load_adj(g, slot):
                sp.dma_start(adj_ring[:, slot], adj[g].rearrange("(p t) n -> p t n", t=T)).then_inc(s["adj_in"], 16)

            sp.dma_start(Wp[:, :, 0:D], W_proj.rearrange("(k p) o -> p k o", p=P)).then_inc(s["w_in"], 16)
            sp.dma_start(Watt[:, :, :, :].rearrange("p h c k -> p (h c k)"),
                         W_att.rearrange("h k -> (h k)").partition_broadcast(P)).then_inc(s["att_in"], 16)
            sp.dma_start(batt[:, :], b_att.partition_broadcast(P)).then_inc(s["att_in"], 16)
            load_x(0, 0)
            load_adj(0, 0)
            sp.dma_start(insr[:, :], ins_tk[0]).then_inc(s["small_in"], 16)
            sp.dma_start(gate[:, :, :], gate_w.rearrange("(k p) e -> p k e", p=P)).then_inc(s["small_in"], 16)
            sp.dma_start(rmod[:, :, :], rmod_w.rearrange("(k p) e -> p k e", p=P)).then_inc(s["small_in"], 16)
            sp.dma_start(gammaT[:, :, :], gamma_t.rearrange("(k p) e -> p k e", p=P)).then_inc(s["small_in"], 16)
            sp.dma_start(expb[:, :], expert_b).then_inc(s["small_in"], 16)
            for k in range(K):
                sp.dma_start(big[:, k], expert_w[:, k * P:(k + 1) * P].rearrange("e p d -> p e d")).then_inc(s["exp_in"], 16)
            for k in range(K):
                sp.dma_start(beta_sb[:, k], beta_w[:, k * P:(k + 1) * P].rearrange("e p d -> p e d")).then_inc(s["beta_in"], 16)

            def body(par, a, b, r, c, d, f):
                if a is not None and not (isinstance(a, int) and a + 1 == G):
                    sp.wait_ge(s["x_in"], (a + 1) * 16)
                    load_x(a + 1, (a + 1) % RING)
                    sp.wait_ge(s["adj_in"], (a + 1) * 16)
                    if not isinstance(a, int) or a >= 1:
                        sp.wait_ge(s["a_mb"], a)
                    load_adj(a + 1, 1 - par)
                if a is not None:
                    sp.wait_ge(s["a_row"], a + 1)
                    if isinstance(a, int) and a == 0:
                        sp.wait_ge(s["bet_mm"], 1)
                    sp.dma_start(row_dram[par].rearrange("(h i) -> h i", h=H), arow[:, :]).then_inc(s["row_out"], 16)
                    sp.wait_ge(s["row_out"], (a + 1) * 16)
                    sp.dma_start(abc[:, par], row_dram[par].partition_broadcast(P)).then_inc(s["abc_in"], 16)
                if f is not None:
                    sp.wait_ge(s["f_fin"], f + 1)
                    sp.dma_start(out[f].rearrange("(p t) d -> p t d", t=T), acc2[:, 1 - par]).then_inc(s["f_out"], 16)

            with sp.If(fast_path(sp) == 1):
                iterations(sp, body, G - 2)
                sp.wait_ge(s["f_out"], G * 16)
            with sp.Else():
                sp.sem_inc(s["out_d"], 16)
                sp.wait_ge(s["bet_mm"], 1)
                for first, last in ((1, AR), (AR, G)):
                    with sp.Fori(first, last) as g:
                        sp.wait_ge(s["x_in"], g * 16)
                        load_x(g, g)
                        sp.wait_ge(s["w_in"], 16)
                        sp.wait_ge(s["adj_in"], g * 16)
                        if first == AR:
                            sp.wait_ge(s["mask1"], (g - AR + 1) * T)
                        load_adj(g, g % AR)
                with sp.Fori(0, G) as g:
                    sp.wait_ge(s["e_acc"], (g + 1) * T * E)
                    sp.dma_start(out[g].rearrange("(p t) d -> p t d", t=T), acc[:, :, :]).then_inc(s["out_d"], 16)
                sp.wait_ge(s["out_d"], (G + 1) * 16)

        @block.gpsimd
        def _(pool):
            pool.memset(ident[:, :], 0.0).then_inc(s["id_zero"], 1)
            pool.memset(eye[:, :, :], 0.0).then_inc(s["id_zero"], 1)
            pool.memset(rowsel[:, :], 1.0).then_inc(s["id_zero"], 1)
            pool.memset(ones[:, :], 1.0).then_inc(s["consts"], 1)
            pool.memset(mean_w[:, :], 1.0 / N).then_inc(s["consts"], 1)
            pool.memset(mhalf[:, :], -0.5).then_inc(s["consts"], 1)
            pool.memset(ninv[:, :], 1.0 / NI).then_inc(s["consts"], 1)
            pool.memset(vals[:, :, :], SENTINEL).then_inc(s["consts"], 1)
            pool.memset(lg[:, :, :], SENTINEL).then_inc(s["consts"], 1)
            pool.memset(xh1[:, :, :, :, KH], 1.0).then_inc(s["consts"], 1)
            pool.wait_ge(s["id_zero"], 3)
            pool.affine_select(out=ident[:, :], in_=ident[:, :], compare_op=ALU.not_equal, fill=1.0, base=0,
                               pattern=[[-1, P]], channel_multiplier=1).then_inc(s["id_one"], 1)
            pool.affine_select(out=eye[:, :, :], in_=eye[:, :, :], compare_op=ALU.not_equal, fill=1.0, base=0,
                               pattern=[[1, E], [-1, E]], channel_multiplier=0).then_inc(s["id_one"], 1)
            pool.affine_select(out=rowsel[:, 0:1], in_=rowsel[:, 0:1], compare_op=ALU.is_gt, fill=0.0, base=2 * E,
                               pattern=[[0, 1]], channel_multiplier=-1).then_inc(s["id_one"], 1)
            pool.affine_select(out=rowsel[:, 1:2], in_=rowsel[:, 1:2], compare_op=ALU.is_ge, fill=0.0, base=-2 * E,
                               pattern=[[0, 1]], channel_multiplier=1).then_inc(s["id_one"], 1)
            pool.wait_ge(s["id_one"], 4)
            pool.tensor_copy(ident16[:, :], ident[:, :]).then_inc(s["eye16"], 1)

            def rsqrt(pre, g, m, v, o):
                held(pool, pre + "_mv", (g + 1) * T)
                pool.tensor_scalar(v[:, :], m[:, :, 1], EPS, 1.0, ALU.add, ALU.mult).then_inc(s[pre + "_var"], 1)
                pool.wait_ge(s[pre + "_var"], g + 1)
                pool.tensor_tensor(o[:, :], v[:, :], mhalf[:, :], ALU.pow).then_inc(s[pre + "_rstd"], 1)

            def fold(t, g, q, n):
                y = ybuf[:, 3 * t:3 * t + 3]
                if n == 0:
                    pool.wait_ge(s["d_act"], g * 6 + (3 if t == 0 else 5))
                    pool.tensor_tensor(y[:, 0], y[:, 0], y[:, 1], ALU.add).then_inc(s["d_pool"], 1)
                if n == 1:
                    pool.wait_ge(s["d_act"], g * 6 + (4 if t == 0 else 6))
                    pool.wait_ge(s["d_pool"], g * 6 + 3 * t + 1)
                    pool.tensor_tensor(y[:, 0], y[:, 0], y[:, 2], ALU.add).then_inc(s["d_pool"], 1)
                    pool.wait_ge(s["d_pool"], g * 6 + 3 * t + 2)
                    pool.tensor_tensor(yfold[:, q, t, :], y[:, 0, 0, :], y[:, 0, 1, :], ALU.add).then_inc(s["d_pool"], 1)

            def body(par, a, b, r, c, d, f):
                other = 1 - par
                xe_t = xe[:, :, :, :, :].rearrange("p t h c k -> p t (h c k)")

                def weighed():
                    pool.wait_ge(s["a_ev"], (b + 1) * T)
                    pool.wait_ge(s["a_beta"], b + 1)
                    pool.tensor_tensor(xe[:, :, :, :, :].rearrange("p t h c k -> p (t h) c k"),
                                       xh1[:, other].rearrange("p t h k -> p (t h) k").unsqueeze(2).broadcast_to([P, T * H, 2, X1]),
                                       beta2[:, :, :, :].rearrange("p t h c -> p (t h) c").unsqueeze(3).broadcast_to([P, T * H, 2, X1]),
                                       ALU.mult).then_inc(s["b_xe"], 1)

                def quotient(t):
                    pool.wait_ge(s["r_rd"], r * T + t + 1)
                    pool.tensor_tensor(oo[:, t, :].rearrange("p (h k) -> p h k", h=H), nn[:, t, :, 0:KH],
                                       rden[:, t, :].unsqueeze(2).broadcast_to([P, H, KH]), ALU.mult).then_inc(s["r_o"], 1)

                if a is not None:
                    rsqrt("a", a, mv, vare, rstd)
                if c is not None:
                    rsqrt("c", c, mv2, vare2, rstd2)
                if b is not None:
                    weighed()
                if f is not None:
                    fold(1, f, other, 1)
                if r is not None:
                    quotient(0)
                if b is not None:
                    pool.wait_ge(s["b_p0"], b + 1)
                    pool.tensor_tensor(xe_t, xe_t, xp[:, other, :, 0, :], ALU.subtract).then_inc(s["b_r"], 1)
                if d is not None:
                    fold(0, d, par, 0)
                if b is not None:
                    pool.wait_ge(s["b_p1"], b + 1)
                    pool.tensor_tensor(xp[:, other, :, 2, :], xe_t, xp[:, other, :, 1, :], ALU.subtract).then_inc(s["b_p2"], 1)
                if r is not None:
                    quotient(1)
                if d is not None:
                    fold(0, d, par, 1)
                    fold(1, d, par, 0)

            with pool.If(fast_path(pool) == 1):
                iterations(pool, body)
            with pool.Else():
                with pool.Fori(0, G) as g:
                    mv_done = pool.to_reg((g + 1) * T)
                    pool.wait_ge(s["id_zero"], 2)
                    pool.wait_ge(s["mv_d"], mv_done)
                    pool.tensor_scalar(vare[:, :], mv[:, :, 1], EPS, None, ALU.add).then_inc(s["vare_d"], 1)
                    pool.wait_ge(s["vare_d"], g + 1)
                    pool.tensor_tensor(rstd[:, :], vare[:, :], mhalf[:, :], ALU.pow).then_inc(s["rstd_d"], 1)
                with pool.Fori(0, G) as g:
                    mv_done = pool.to_reg((g + 1) * T)
                    pool.wait_ge(s["id_zero"], 2)
                    pool.wait_ge(s["fmv_d"], mv_done)
                    pool.tensor_scalar(vare[:, :], mv[:, :, 1], EPS, None, ALU.add).then_inc(s["fvare_d"], 1)
                    pool.wait_ge(s["fvare_d"], g + 1)
                    pool.tensor_tensor(rstd[:, :], vare[:, :], mhalf[:, :], ALU.pow).then_inc(s["frstd_d"], 1)

        @block.scalar
        def _(act):
            act.preload_act_table(ACT.Exp)

            def body(par, a, b, r, c, d, f):
                other = 1 - par

                def scaled(k, y):
                    if d is None:
                        return
                    q, t = (k - 1) // T, (k - 1) % T
                    act.wait_ge(s["d_mm"], d * 9 + k + 1)
                    act.wait_ge(s["c_cmb"], d + 1)
                    if not (isinstance(d, int) and d == 0):
                        act.wait_ge(s["d_pool"], (d - 1) * 6 + 3 * (t + 1))
                    for i in range(2):
                        ins = act.activation(ybuf[:, y, i, :], bE[k % 3][:, i * D:(i + 1) * D], ACT.Copy,
                                             scale=cmb2[:, par, t, 2 * q + i:2 * q + i + 1])
                    ins.then_inc(s["d_act"], 1)

                def evacuate(t):
                    act.wait_ge(s["a_xp"], a * T + t + 1)
                    act.activation(xh1[:, par, t, :, 0:KH], bX[:, 0:D].rearrange("p (h k) -> p h k", h=H), ACT.Copy)
                    act.activation(ab[:, t, :], bX[:, D:D + HA], ACT.Copy).then_inc(s["a_ev"], 1)

                def part(i, ready):
                    act.wait_ge(s[ready], b + 1)
                    act.activation(xp[:, other, :, i, :], xe[:, :, :, :, :].rearrange("p t h c k -> p t (h c k)"),
                                   ACT.Copy).then_inc(s[f"b_p{i}"], 1)

                scaled(1, 0)
                if b is not None:
                    if not (isinstance(b, int) and b < 2):
                        act.wait_ge(s["r_t0"], (b - 1) * T)
                    act.wait_ge(s["a_neg"], b + 1)
                    act.activation(rho[:, other].rearrange("p t h -> p (t h)"), asrc2[:, other].rearrange("p t h -> p (t h)"),
                                   ACT.Exp, scale=1.0 - SLOPE).then_inc(s["b_rho"], 1)
                if a is not None:
                    act.wait_ge(s["a_xT"], a + 1)
                    act.activation(xTh[:, :, :, :].rearrange("p k t n -> p (k t n)"), bT[:, :], ACT.Copy).then_inc(s["a_hi"], 1)
                if b is not None:
                    part(0, "b_xe")
                scaled(2, 3)
                if a is not None:
                    evacuate(0)
                if c is not None:
                    act.wait_ge(s["c_xT"], c + 1)
                    act.activation(fTh[:, other].rearrange("p k t n -> p (k t n)"), bT[:, :], ACT.Copy).then_inc(s["c_hi"], 1)
                if a is not None:
                    act.wait_ge(s["a_mT"], a + 1)
                    act.activation(mtn[:, par].rearrange("p u i -> p (u i)"), bS[:, 0:N].bitcast(BF16), ACT.Copy,
                                   scale=-1.0).then_inc(s["a_mneg"], 1)
                scaled(3, 1)
                if a is not None:
                    evacuate(1)
                if b is not None:
                    part(1, "b_r")
                if c is not None:
                    act.wait_ge(s["c_lT"], c + 1)
                    act.activation(lgT[:, :], bS[0:E, 0:N], ACT.Copy).then_inc(s["c_lTs"], 1)
                if a is not None:
                    act.wait_ge(s["a_ev"], (a + 1) * T)
                    act.activation(beta2[:, :, :, 0], ab[:, :, H:HA], ACT.Exp)
                    act.activation(beta2[:, :, :, 1], ab[:, :, H:HA], ACT.Exp, scale=SLOPE).then_inc(s["a_beta"], 1)
                    act.wait_ge(s["a_rT"], a + 1)
                    if not (isinstance(a, int) and a == 0):
                        act.wait_ge(s["row_out"], a * 16)
                    act.activation(arow[:, :], bS[0:H, 0:N], ACT.Copy).then_inc(s["a_row"], 1)
                if b is not None:
                    act.wait_ge(s["b_S"], b + 1)
                    act.activation(sbc[:, other, :], bX[:, 0:D], ACT.Copy).then_inc(s["b_Sb"], 1)
                scaled(5, 2)
                if c is not None:
                    act.wait_ge(s["c_lgm"], c + 1)
                    act.activation(ex[:, :, :].rearrange("p t e -> p (t e)"), lgm[:, :, :].rearrange("p t e -> p (t e)"),
                                   ACT.Exp).then_inc(s["c_ex"], 1)
                scaled(6, 4)
                if c is not None:
                    act.wait_ge(s["c_cT"], c + 1)
                    act.activation(cT3[:, other].rearrange("e t n -> e (t n)"), bS[0:3 * E, 0:N], ACT.Copy).then_inc(s["c_cTs"], 1)
                scaled(8, 5)

            with act.If(fast_path(act) == 1):
                iterations(act, body)
            with act.Else():
                with act.Fori(0, G) as g:
                    act.wait_ge(s["xT_mm"], g + 1)
                    act.activation(xTh[:, :, :, :].rearrange("p k t n -> p (k t n)"), pT[:, :], ACT.Copy).then_inc(s["xTh_d"], 1)
                    act.wait_ge(s["xp_mm"], (g + 1))
                    for t, bk in enumerate((pA, pB)):
                        act.activation(xh[:, t, :], bk[:, 0:D], ACT.Copy).then_inc(s["xh_d"], 1)
                    for n in range(T * H):
                        act.wait_ge(s["l_d"], g * T * H + n + 1)
                        act.activation(prob[:, :], lsc[:, :], ACT.Exp, bias=rmax[:, 3:4], accum_out=psum_row[:, :]).then_inc(s["prob_d"], 1)
                        act.wait_ge(s["pT_mm"], g * T * H + n + 1)
                        act.activation(probT[:, :, :].rearrange("p t n -> p (t n)"), pT[:, 0:N], ACT.Copy).then_inc(s["pT_d"], 1)
                with act.Fori(0, G) as g:
                    act.wait_ge(s["fxT_mm"], g + 1)
                    act.activation(xTh[:, :, :, :].rearrange("p k t n -> p (k t n)"), pT[:, :], ACT.Copy).then_inc(s["fxTh_d"], 1)
                    for t in range(T):
                        act.wait_ge(s["nmx_d"], g * T + t + 1)
                        act.activation(ex[:, t, :], lg[:, t, 0:E], ACT.Exp, bias=nmx[:, t:t + 1], accum_out=exs[:, t:t + 1]).then_inc(s["ex_d"], 1)
                    act.wait_ge(s["cT_mm"], g + 1)
                    act.activation(cT[:, :, :].rearrange("e t n -> e (t n)"), pB[0:E, 0:N], ACT.Copy).then_inc(s["cT_d"], 1)

        @block.vector
        def _(dve):
            dve.wait_ge(s["w_in"], 16)
            dve.wait_ge(s["att_in"], 32)
            n = 0
            for k in range(K):
                for c in range(2):
                    if n:
                        dve.wait_ge(s["watt_sum"], n)
                    dve.tensor_tensor(wprod[:, :, :], Wp[:, k, 0:D].rearrange("p (h k) -> p h k", h=H), Watt[:, :, c, :],
                                      ALU.mult).then_inc(s["watt_prod"], 1)
                    n += 1
                    dve.wait_ge(s["watt_prod"], n)
                    dve.tensor_reduce(Wp[:, k, D + c * H:D + (c + 1) * H], wprod[:, :, :], AX.X, ALU.add).then_inc(s["watt_sum"], 1)
            dve.wait_ge(s["watt_sum"], n)
            dve.tensor_tensor(wsq[:, :, :], Wp[:, :, D:D + HA], Wp[:, :, D:D + HA], ALU.mult).then_inc(s["wsq_d"], 1)
            dve.tensor_copy(Wph[:, :, :], Wp[:, :, :]).then_inc(s["wp_hi"], 1)
            dve.wait_ge(s["wp_hi"], 1)
            dve.tensor_tensor(Wpl[:, :, :], Wp[:, :, :], Wph[:, :, :].bitcast(F32), ALU.subtract).then_inc(s["wp_lo"], 1)
            dve.wait_ge(s["wsq_mm"], 1)
            dve.tensor_reduce(bnd[:, 0:1], bX[:, 0:HA], AX.X, ALU.max).then_inc(s["bnd_max"], 1)
            dve.tensor_reduce(bnd[:, 1:2], batt[:, :], AX.X, ALU.max, apply_absolute_value=True).then_inc(s["bnd_max"], 1)
            dve.wait_ge(s["bnd_max"], 2)
            dve.tensor_scalar(bnd[:, 2:3], bnd[:, 0:1], BOUND * BOUND / D, None, ALU.is_le).then_inc(s["bnd_ok"], 1)
            dve.tensor_scalar(bnd[:, 3:4], bnd[:, 1:2], BOUND, None, ALU.is_le).then_inc(s["bnd_ok"], 1)
            dve.wait_ge(s["bnd_ok"], 2)
            dve.tensor_tensor(flag[:, :], bnd[:, 2:3], bnd[:, 3:4], ALU.mult).then_inc(s["flag_d"], 1)

            dve.wait_ge(s["small_in"], 16 * 5)
            dve.tensor_copy(gateh[:, :, :], gate[:, :, :]).then_inc(s["gate_hi"], 1)
            dve.wait_ge(s["gate_hi"], 1)
            dve.tensor_tensor(gatel[:, :, :], gate[:, :, :], gateh[:, :, :].bitcast(F32), ALU.subtract).then_inc(s["gate_lo"], 1)
            dve.wait_ge(s["insm_mm"], 1)
            dve.tensor_copy(insm[:, :], bS[:, 0:K]).then_inc(s["insm_sb"], 1)
            dve.wait_ge(s["mod_mm"], 1)
            dve.tensor_copy(gam_all[:, :], bS[:, 16:16 + E]).then_inc(s["mod_sb"], 1)
            dve.tensor_copy(rgam[:, :], bS[:, 32:32 + E]).then_inc(s["mod_sb"], 1)
            dve.tensor_copy(gam_col[:, :], bS[0:E, 48:49]).then_inc(s["mod_sb"], 1)
            dve.wait_ge(s["mod_sb"], 3)
            dve.wait_ge(s["id_one"], 4)
            for k in range(K):
                dve.tensor_scalar(insd[:, k], eye[:, :, :].unsqueeze(2).broadcast_to([P, E, 3, E]), insm[:, k:k + 1], None,
                                  ALU.mult).then_inc(s["diag"], 1)
            dve.tensor_scalar(gamd[:, :, :], ident[0:E, 0:E].unsqueeze(1).broadcast_to([E, 3, E]), gam_col[:, 0:1], None,
                              ALU.mult).then_inc(s["diag"], 1)

            def expert_parts():
                dve.wait_ge(s["exp_in"], 16 * K)
                for e in range(E):
                    dve.tensor_scalar(big[:, :, e, :], big[:, :, e, :], gam_all[:, e:e + 1], None, ALU.mult).then_inc(s["exp_scaled"], 1)
                dve.wait_ge(s["exp_scaled"], E)
                dve.tensor_copy(Weh[:, :, :, :], big[:, :, :, :]).then_inc(s["exp_hi"], 1)
                dve.wait_ge(s["exp_hi"], 1)
                dve.tensor_tensor(Wel[:, :, :, :], big[:, :, :, :], Weh[:, :, :, :].bitcast(F32), ALU.subtract).then_inc(s["exp_lo"], 1)

            def v_rows():
                dve.wait_ge(s["bet_mm"], 1)
                dve.tensor_copy(Vr[:, :], bE[0][0:3 * E, 0:D]).then_inc(s["v_raw"], 1)
                dve.wait_ge(s["v_raw"], 1)
                dve.tensor_copy(Vh[:, :], Vr[:, :]).then_inc(s["v_hi"], 1)
                dve.wait_ge(s["v_hi"], 1)
                dve.tensor_tensor(Vl[:, :], Vr[:, :], Vh[:, :].bitcast(F32), ALU.subtract).then_inc(s["v_lo"], 1)
                dve.wait_ge(s["v_lo"], 1)
                dve.tensor_scalar(Vl[:, :], Vl[:, :], rowsel[:, 1:2], None, ALU.mult).then_inc(s["v_sel"], 1)
                dve.wait_ge(s["v_sel"], 1)
                dve.scalar_tensor_tensor(V3[:, :], Vh[:, :].bitcast(F32), rowsel[:, 0:1], Vl[:, :], ALU.mult, ALU.add).then_inc(s["v_sb"], 1)

            def body(par, a, b, r, c, d, f):
                other = 1 - par

                def targets(h):
                    if b is None:
                        return
                    if h == 0:
                        dve.wait_ge(s["abc_in"], (b + 1) * 16)
                        dve.wait_ge(s["a_mneg"], b + 1)
                    for u in range(T):
                        dve.scalar_tensor_tensor(Q[:, other, u, h, :], abc[:, other, h * N:(h + 1) * N],
                                                 negb[:, other, u, h:h + 1], mtn[:, other, u, :], ALU.is_gt, ALU.mult).then_inc(s["b_q"], 1)

                def experts(k, last):
                    if d is None:
                        return
                    q, t = (k - 1) // T, (k - 1) % T
                    dve.wait_ge(s["d_mm"], d * 9 + k + 1)
                    dve.wait_ge(s["d_dve"], d * 3 + 1)
                    dve.scalar_tensor_tensor(acc2[:, par, t, :], bE[k % 3][:, 0:D], cmb2[:, par, t, 2 * q:2 * q + 1],
                                             acc2[:, par, t, :], ALU.mult, ALU.add).then_inc(s["d_link"], 1)
                    dve.wait_ge(s["d_link"], d * 2 + last)
                    dve.scalar_tensor_tensor(acc2[:, par, t, :], bE[k % 3][:, D:2 * D], cmb2[:, par, t, 2 * q + 1:2 * q + 2],
                                             acc2[:, par, t, :], ALU.mult, ALU.add).then_inc(s["d_dve"], 1)

                def row_sums(t):
                    if r is None:
                        return
                    i = r * T + t + 1
                    sums = bR[:, :, 0:H // 2 * 2 * X1].rearrange("p f (h c) -> p f h c", c=2 * X1)
                    halves = nt[:, t].rearrange("p (f h) k -> p f h k", f=2)
                    dve.wait_ge(s["r_mm"], i)
                    dve.wait_ge(s["b_rho"], r + 1)
                    dve.tensor_tensor(halves, sums[:, :, :, 0:X1],
                                      rho[:, par, t, :].rearrange("p (f h) -> p f h", f=2).unsqueeze(3).broadcast_to([P, 2, H // 2, X1]),
                                      ALU.mult).then_inc(s["r_t0"], 1)
                    dve.wait_ge(s["r_t0"], i)
                    dve.tensor_tensor(nn[:, t].rearrange("p (f h) k -> p f h k", f=2), sums[:, :, :, X1:2 * X1], halves,
                                      ALU.subtract).then_inc(s["r_n"], 1)

                def row_weights(t):
                    if r is None:
                        return
                    i = r * T + t + 1
                    dve.wait_ge(s["r_n"], i)
                    dve.tensor_scalar(emp[:, t, :], nn[:, t, 0, KH:X1], 0.0, None, ALU.is_equal).then_inc(s["r_e"], 1)
                    dve.wait_ge(s["r_e"], i)
                    dve.tensor_scalar(dsum[:, t, :], nn[:, t, :, KH], emp[:, t, :], None, ALU.add).then_inc(s["r_ds"], 1)
                    dve.wait_ge(s["r_ds"], i)
                    dve.reciprocal(rden[:, t, :], dsum[:, t, :]).then_inc(s["r_rd"], 1)

                def row_out(t):
                    if r is None:
                        return
                    i = r * T + t + 1
                    dve.wait_ge(s["r_o"], i)
                    dve.wait_ge(s["b_Sb"], r + 1)
                    dve.scalar_tensor_tensor(oo[:, t, :], sbc[:, par, :], emp[:, t, :], oo[:, t, :], ALU.mult, ALU.add).then_inc(s["r_z"], 1)
                    dve.wait_ge(s["r_z"], i)
                    dve.scalar_tensor_tensor(x_all[:, r % RING, t, :], oo[:, t, :], 0.0, x_all[:, r % RING, t, :], ALU.max,
                                             ALU.add).then_inc(s["r_x1"], 1)

                def statistics(g, ready, rows, st, m, pre):
                    held(dve, ready, rows)
                    for t in range(T):
                        dve.bn_stats(st[:, t, :], x_all[:, g % RING, t, :]).then_inc(s[pre + "_stats"], 1)
                    held(dve, pre + "_stats", (g + 1) * T)
                    for t in range(T):
                        dve.bn_aggr(m[:, t, :], st[:, t, :]).then_inc(s[pre + "_mv"], 1)

                def normalise(g, to, m, rs, pre):
                    dve.wait_ge(s[pre + "_rstd"], g + 1)
                    for t in range(T):
                        dve.tensor_scalar(to[:, t, :], x_all[:, g % RING, t, :], m[:, t, 0:1], rs[:, t:t + 1], ALU.subtract,
                                          ALU.mult).then_inc(s[pre + "_xn"], 1)

                def lower(g, hi, lo, pre):
                    dve.wait_ge(s[pre + "_hi"], g + 1)
                    dve.tensor_tensor(lo.rearrange("p k t n -> p (k t n)"), bT[:, :],
                                      hi.rearrange("p k t n -> p (k t n)").bitcast(F32), ALU.subtract).then_inc(s[pre + "_lo"], 1)

                def neighbour_mask():
                    dve.wait_ge(s["adj_in"], (a + 1) * 16)
                    for t in range(T):
                        ins = dve.tensor_scalar(mb[:, t], adj_ring[:, par, t, :].rearrange("p (q u) -> p u q", u=T), 0, None, ALU.is_gt)
                    ins.then_inc(s["a_mb"], 1)

                def source_terms():
                    dve.wait_ge(s["a_ev"], (a + 1) * T)
                    dve.tensor_tensor(asrc2[:, par], ab[:, :, 0:H], batt[:, :].unsqueeze(1).broadcast_to([P, T, H]),
                                      ALU.add).then_inc(s["a_src"], 1)
                    dve.tensor_scalar(negb[:, par], ab[:, :, H:HA], -1.0, None, ALU.mult).then_inc(s["a_neg"], 1)

                def base():
                    dve.wait_ge(s["d_mm"], d * 9 + 1)
                    if not (isinstance(d, int) and d <= 1):
                        dve.wait_ge(s["f_out"], (d - 1) * 16)
                    dve.tensor_tensor(acc2[:, par], bE[0][:, :].rearrange("p (t d) -> p t d", t=T), x_all[:, d % RING],
                                      ALU.add).then_inc(s["d_dve"], 1)

                def best_two():
                    dve.wait_ge(s["c_lb"], c + 1)
                    dve.tensor_tensor(lg[:, :, 0:E], bS[:, 0:T * E].rearrange("p (t e) -> p t e", t=T),
                                      rgam[:, :].unsqueeze(1).broadcast_to([P, T, E]), ALU.add).then_inc(s["c_lg"], 1)
                    held(dve, "c_lg", c + 1)
                    for t in range(T):
                        dve.max(m8[:, t, :], lg[:, t, 0:E]).then_inc(s["c_m8"], 1)
                    dve.wait_ge(s["c_m8"], (c + 1) * T)
                    dve.tensor_tensor(lgm[:, :, :], lg[:, :, 0:E], m8[:, :, 0:1].broadcast_to([P, T, E]), ALU.subtract).then_inc(s["c_lgm"], 1)
                    dve.tensor_copy(vals[:, :, 0:2], m8[:, :, 0:2]).then_inc(s["c_vals"], 1)

                def combine():
                    held(dve, "c_vals", c + 1)
                    for t in range(T):
                        dve.match_replace(rep[:, t, 0:14], vals[:, t, :], lg[:, t, 0:14], SENTINEL).then_inc(s["c_rep"], 1)
                    dve.wait_ge(s["c_ex"], c + 1)
                    dve.tensor_reduce(exs[:, :], ex[:, :, :], AX.X, ALU.add).then_inc(s["c_sum"], 1)
                    dve.wait_ge(s["c_rep"], (c + 1) * T)
                    dve.tensor_tensor(sel[:, :, :], rep[:, :, 0:E], lg[:, :, 0:E], ALU.not_equal).then_inc(s["c_sel"], 1)
                    dve.wait_ge(s["c_sum"], c + 1)
                    dve.reciprocal(rex[:, :], exs[:, :]).then_inc(s["c_rec"], 1)
                    dve.wait_ge(s["c_sel"], c + 1)
                    dve.tensor_tensor(exsel[:, :, :], ex[:, :, :], sel[:, :, :], ALU.mult).then_inc(s["c_es"], 1)
                    dve.wait_ge(s["c_es"], c + 1)
                    dve.wait_ge(s["c_rec"], c + 1)
                    dve.tensor_tensor(cmb2[:, other], exsel[:, :, :], rex[:, :].unsqueeze(2).broadcast_to([P, T, E]),
                                      ALU.mult).then_inc(s["c_cmb"], 1)
                    dve.wait_ge(s["c_cmb"], c + 1)
                    dve.tensor_copy(c3[:, :, 0, :].bitcast(F32R), cmb2[:, other]).then_inc(s["c_ch"], 1)
                    dve.wait_ge(s["c_ch"], c + 1)
                    dve.tensor_tensor(c3[:, :, 1, :], cmb2[:, other], c3[:, :, 0, :], ALU.subtract).then_inc(s["c_cl"], 1)
                    dve.tensor_copy(c3[:, :, 2, :], c3[:, :, 0, :]).then_inc(s["c_c3"], 1)

                if a is not None:
                    statistics(a, "x_in", (a + 1) * 16, stats, mv, "a")
                if c is not None:
                    statistics(c, "r_x1", (c + 1) * T, stats2, mv2, "c")
                if b is not None:
                    dve.wait_ge(s["a_mneg"], b + 1)
                    dve.tensor_scalar(mt[:, other], mtn[:, other], -1.0, None, ALU.mult).then_inc(s["b_mt"], 1)
                if a is not None:
                    normalise(a, xn, mv, rstd, "a")
                if c is not None:
                    normalise(c, xf, mv2, rstd2, "c")
                if a is not None:
                    neighbour_mask()
                targets(0)
                if d is not None:
                    base()
                if a is not None:
                    lower(a, xTh[:, :, :, :], xTl[:, :, :, :], "a")
                row_sums(0)
                row_weights(0)
                targets(1)
                if c is not None:
                    lower(c, fTh[:, other], fTl[:, other], "c")
                row_out(0)
                targets(2)
                if a is not None:
                    source_terms()
                if f is not None:
                    dve.wait_ge(s["d_pool"], (f + 1) * 6)
                    dve.wait_ge(s["d_dve"], (f + 1) * 3)
                    dve.tensor_tensor(acc2[:, other], acc2[:, other], yfold[:, other], ALU.add).then_inc(s["f_fin"], 1)
                targets(3)
                targets(4)
                experts(4, 1)
                row_sums(1)
                row_weights(1)
                targets(5)
                if c is not None:
                    best_two()
                targets(6)
                if c is not None:
                    combine()
                row_out(1)
                experts(7, 2)
                targets(7)
                if isinstance(a, int) and a == 0:
                    expert_parts()
                    v_rows()

            with dve.If(fast_path(dve) == 1):
                iterations(dve, body)
            with dve.Else():
                expert_parts()
                v_rows()
                with dve.Fori(0, G) as g:
                    dve.wait_ge(s["x_in"], (g + 1) * 16)
                    for t in range(T):
                        dve.bn_stats(stats[:, t, :], x_all[:, g, t, :]).then_inc(s["stats_d"], 1)
                    for t in range(T):
                        stats_done = dve.to_reg(g * T + t + 1)
                        dve.wait_ge(s["id_one"], 2)
                        dve.wait_ge(s["stats_d"], stats_done)
                        dve.bn_aggr(mv[:, t, :], stats[:, t, :]).then_inc(s["mv_d"], 1)
                    dve.wait_ge(s["rstd_d"], g + 1)
                    for t in range(T):
                        dve.tensor_scalar(xn[:, t, :], x_all[:, g, t, :], mv[:, t, 0:1], rstd[:, t:t + 1], ALU.subtract,
                                          ALU.mult).then_inc(s["xn_d"], 1)
                    dve.wait_ge(s["xTh_d"], g + 1)
                    dve.tensor_tensor(xTl[:, :, :, :].rearrange("p k t n -> p (k t n)"), pT[:, :],
                                      xTh[:, :, :, :].rearrange("p k t n -> p (k t n)").bitcast(F32), ALU.subtract).then_inc(s["xTl_d"], 1)
                    dve.wait_ge(s["xh_d"], (g + 1) * T)
                    for t, bk in enumerate((pA, pB)):
                        dve.tensor_tensor(asrc[:, t, :], bk[:, D:D + H], batt[:, :], ALU.add).then_inc(s["asrc_d"], 1)
                        dve.tensor_copy(adst[:, t, :], bk[:, D + H:D + HA]).then_inc(s["adst_d"], 1)
                    dve.wait_ge(s["adj_in"], (g + 1) * 16)
                    for t in range(T):
                        dve.tensor_scalar(mbias[:, t, :].rearrange("p (u q) -> p u q", u=T),
                                          adj_ring[:, g % AR, t, :].rearrange("p (q u) -> p u q", u=T), 0, None, ALU.is_gt).then_inc(s["mask1"], 1)
                    dve.wait_ge(s["mask1"], (g + 1) * T)
                    dve.tensor_scalar(mbias[:, :, :], mbias[:, :, :], -MASKED, MASKED, ALU.mult, ALU.add).then_inc(s["mask2"], 1)
                    dve.wait_ge(s["mask2"], g + 1)
                    dve.wait_ge(s["asrc_d"], (g + 1) * T)
                    for n in range(T * H):
                        t, h = n // H, n % H
                        i = dve.to_reg(g * T * H + n + 1)
                        dve.wait_ge(s["id_one"], 2)
                        dve.wait_ge(s["bc_mm"], i)
                        dve.tensor_tensor_reduce(vsc[:, :], pC[:, 0:N], mbias[:, t, :], 1.0, -3e38, ALU.add, ALU.max,
                                                 rmax[:, 0:1]).then_inc(s["vmax_d"], 1)
                        dve.wait_ge(s["vmax_d"], i)
                        dve.tensor_scalar(rmax[:, 1:2], rmax[:, 0:1], asrc[:, t, h:h + 1], None, ALU.add).then_inc(s["top1"], 1)
                        dve.tensor_scalar(vsc[:, :], vsc[:, :], asrc[:, t, h:h + 1], None, ALU.add).then_inc(s["t_d"], 1)
                        dve.wait_ge(s["top1"], i)
                        dve.scalar_tensor_tensor(rmax[:, 2:3], rmax[:, 1:2], SLOPE, rmax[:, 1:2], ALU.mult, ALU.max).then_inc(s["top2"], 1)
                        dve.wait_ge(s["t_d"], i)
                        dve.scalar_tensor_tensor(lsc[:, :], vsc[:, :], SLOPE, vsc[:, :], ALU.mult, ALU.max)
                        dve.wait_ge(s["top2"], i)
                        dve.tensor_scalar(rmax[:, 3:4], rmax[:, 2:3], -1.0, None, ALU.mult).then_inc(s["l_d"], 1)
                        dve.wait_ge(s["prob_d"], i)
                        dve.reciprocal(rrow[:, :], psum_row[:, :]).then_inc(s["rrow_d"], 1)
                        dve.wait_ge(s["rrow_d"], i)
                        dve.wait_ge(s["o_mm"], i)
                        dve.tensor_scalar(att[:, t, h * KH:(h + 1) * KH], pA[:, 0:KH], rrow[:, :], None, ALU.mult).then_inc(s["att_d"], 1)
                    dve.wait_ge(s["att_d"], (g + 1) * T * H)
                    dve.scalar_tensor_tensor(x_all[:, g], att[:, :, :], 0.0, x_all[:, g], ALU.max, ALU.add).then_inc(s["x1_d"], 1)

                with dve.Fori(0, G) as g:
                    dve.wait_ge(s["x1_d"], g + 1)
                    for t in range(T):
                        dve.bn_stats(stats[:, t, :], x_all[:, g, t, :]).then_inc(s["fstats_d"], 1)
                    for t in range(T):
                        stats_done = dve.to_reg(g * T + t + 1)
                        dve.wait_ge(s["id_one"], 2)
                        dve.wait_ge(s["fstats_d"], stats_done)
                        dve.bn_aggr(mv[:, t, :], stats[:, t, :]).then_inc(s["fmv_d"], 1)
                    dve.wait_ge(s["frstd_d"], g + 1)
                    for t in range(T):
                        dve.tensor_scalar(xn[:, t, :], x_all[:, g, t, :], mv[:, t, 0:1], rstd[:, t:t + 1], ALU.subtract,
                                          ALU.mult).then_inc(s["fxn_d"], 1)
                    dve.wait_ge(s["fxTh_d"], g + 1)
                    dve.tensor_tensor(xTl[:, :, :, :].rearrange("p k t n -> p (k t n)"), pT[:, :],
                                      xTh[:, :, :, :].rearrange("p k t n -> p (k t n)").bitcast(F32), ALU.subtract).then_inc(s["fxTl_d"], 1)
                    dve.wait_ge(s["lg_mm"], g + 1)
                    dve.wait_ge(s["consts"], 7)
                    for t in range(T):
                        dve.tensor_tensor(lg[:, t, 0:E], pA[:, t * E:(t + 1) * E], rgam[:, :], ALU.add).then_inc(s["lg_d"], 1)
                    for t in range(T):
                        i = dve.snap(g * T + t + 1)
                        dve.wait_ge(s["id_one"], 2)
                        dve.wait_ge(s["lg_d"], i)
                        dve.max(m8[:, t, :], lg[:, t, 0:E]).then_inc(s["m8_d"], 1)
                        dve.wait_ge(s["m8_d"], i)
                        dve.tensor_scalar(nmx[:, t:t + 1], m8[:, t, 0:1], -1.0, None, ALU.mult).then_inc(s["nmx_d"], 1)
                        dve.tensor_copy(vals[:, t, 0:2], m8[:, t, 0:2]).then_inc(s["vals_d"], 1)
                        dve.wait_ge(s["id_one"], 2)
                        dve.wait_ge(s["vals_d"], i)
                        dve.match_replace(rep[:, t, 0:14], vals[:, t, :], lg[:, t, 0:14], SENTINEL).then_inc(s["rep_d"], 1)
                        dve.wait_ge(s["rep_d"], i)
                        dve.tensor_tensor(sel[:, t, :], rep[:, t, 0:E], lg[:, t, 0:E], ALU.not_equal).then_inc(s["sel_d"], 1)
                        dve.wait_ge(s["ex_d"], i)
                        dve.reciprocal(rex[:, t:t + 1], exs[:, t:t + 1]).then_inc(s["rex_d"], 1)
                        dve.wait_ge(s["rex_d"], i)
                        dve.wait_ge(s["sel_d"], i)
                        dve.scalar_tensor_tensor(cmb[:, t, :], ex[:, t, :], rex[:, t:t + 1], sel[:, t, :], ALU.mult, ALU.mult).then_inc(s["cmb_d"], 1)
                    dve.wait_ge(s["v_mm"], g + 1)
                    dve.wait_ge(s["out_d"], (g + 1) * 16)
                    dve.tensor_tensor(acc[:, :, :], pC[:, :].rearrange("p (t d) -> p t d", t=T), x_all[:, g], ALU.add).then_inc(s["base_d"], 1)
                    dve.wait_ge(s["base_d"], g + 1)
                    dve.wait_ge(s["cmb_d"], (g + 1) * T)
                    for n in range(T * E):
                        e, t = n // (2 * T) * 2 + n % 2, n // 2 % T
                        b = n // 2
                        dve.wait_ge(s["e_mm"], g * T * E // 2 + b + 1)
                        if n:
                            dve.wait_ge(s["e_acc"], g * T * E + n)
                        dve.scalar_tensor_tensor(acc[:, t, :], pE[b % 4][:, (n % 2) * D:(n % 2 + 1) * D], cmb[:, t, e:e + 1],
                                                 acc[:, t, :], ALU.mult, ALU.add).then_inc(s["e_acc"], 1)

        @block.tensor
        def _(pe):
            pe.wait_ge(s["consts"], 7)
            pe.wait_ge(s["id_one"], 4)
            pe.wait_ge(s["eye16"], 1)
            pe.wait_ge(s["wsq_d"], 1)
            for k in range(K):
                mm = pe.matmul(bX[:, 0:HA], ones[:, :], wsq[:, k, :], start=k == 0, stop=k == K - 1)
            mm.then_inc(s["wsq_mm"], 1)
            pe.wait_ge(s["small_in"], 16 * 5)
            for k in range(K):
                mm = pe.matmul(bS[:, k:k + 1], insr[:, k * P:(k + 1) * P], ninv[:, :], start=True, stop=True)
            mm.then_inc(s["insm_mm"], 1)
            pe.wait_ge(s["insm_sb"], 1)
            for k in range(K):
                pe.matmul(bS[:, 16:16 + E], insm[:, k:k + 1].broadcast_to([P, P]), gammaT[:, k, :], start=k == 0, stop=k == K - 1)
            for k in range(K):
                pe.matmul(bS[:, 32:32 + E], insm[:, k:k + 1].broadcast_to([P, P]), rmod[:, k, :], start=k == 0, stop=k == K - 1)
            for k in range(K):
                mm = pe.matmul(bS[0:E, 48:49], gammaT[:, k, :], insm[:, k:k + 1], start=k == 0, stop=k == K - 1)
            mm.then_inc(s["mod_mm"], 1)
            pe.wait_ge(s["wp_lo"], 1)
            pe.wait_ge(s["mod_sb"], 3)
            pe.wait_ge(s["flag_d"], 1)

            def v_rows():
                pe.wait_ge(s["beta_in"], 16 * K)
                pe.wait_ge(s["diag"], K + 1)
                for e in range(E):
                    for k in range(K):
                        pe.matmul(bE[0][0:3 * E, 0:D], insd[:, k, e].rearrange("p a b -> p (a b)"), beta_sb[:, k, e, :],
                                  start=e + k == 0, stop=False)
                pe.matmul(bE[0][0:3 * E, 0:D], gamd[:, :, :].rearrange("p a b -> p (a b)"), expb[:, :], start=False,
                          stop=True).then_inc(s["bet_mm"], 1)

            def body(par, a, b, r, c, d, f):
                other = 1 - par

                def three(out, hi, lo, whi, wlo, first=True, last=True):
                    for k in range(K):
                        for i, (p, w) in enumerate(((hi, whi), (hi, wlo), (lo, whi))):
                            mm = pe.matmul(out, p(k), w(k), start=k == 0 and i == 0, stop=k == K - 1 and i == 2)
                    return mm

                def chunk(k):
                    if d is None:
                        return
                    freed = {0: ("d_act", 5, 1), 1: ("d_dve", 3, 1), 2: ("d_act", 6, 1), 3: ("d_dve", 1, 0),
                             4: ("d_act", 1, 0), 5: ("d_act", 2, 0), 6: ("d_act", 3, 0), 7: ("d_dve", 2, 0), 8: ("d_act", 4, 0)}
                    name, count, back = freed[k]
                    if not (back and isinstance(d, int) and d == 0):
                        pe.wait_ge(s[name], (d - back) * (3 if name == "d_dve" else 6) + count)
                    if k == 0:
                        if isinstance(d, int) and d == 0:
                            pe.wait_ge(s["v_sb"], 1)
                            pe.wait_ge(s["exp_lo"], 1)
                        held(pe, "c_cTs", d + 1)
                        for t in range(T):
                            mm = pe.matmul(bE[0][:, t * D:(t + 1) * D], cT3[:, par, t, :], V3[:, :], start=True, stop=True)
                    else:
                        q, t = (k - 1) // T, (k - 1) % T
                        if k == 1:
                            pe.wait_ge(s["c_lo"], d + 1)
                        mm = three(bE[k % 3][:, :], lambda j: fTh[:, par, j, t, :], lambda j: fTl[:, par, j, t, :],
                                   lambda j: Weh[:, j, 2 * q:2 * q + 2, :].rearrange("p e d -> p (e d)"),
                                   lambda j: Wel[:, j, 2 * q:2 * q + 2, :].rearrange("p e d -> p (e d)"))
                    mm.then_inc(s["d_mm"], 1)

                def neighbours(t, half):
                    if r is None:
                        return
                    if t == 0 and half == 0:
                        pe.wait_ge(s["b_q"], (r + 1) * T * H)
                        pe.wait_ge(s["b_p2"], r + 1)
                    if half == 0 and not (isinstance(r, int) and r * T + t == 0):
                        pe.wait_ge(s["r_n"], r * T + t)
                    for h in range(H // 2 * half, H // 2 * (half + 1)):
                        at = h % (H // 2) * 2 * X1
                        for u in range(T):
                            for i in range(PARTS):
                                pe.matmul(bR[:, half, at:at + 2 * X1], Q[:, par, u, h, t * P:(t + 1) * P],
                                          xp[:, par, u, i, h * 2 * X1:(h + 1) * 2 * X1],
                                          start=at + u + i == 0, stop=False, skip_group_check=True)
                    for u in range(T):
                        for i in range(PARTS):
                            mm = pe.matmul(bR[:, half, 0:H * X1].rearrange("p (h c) -> p h c", c=2 * X1)[:, :, X1:2 * X1],
                                           mt[:, par, u, t * P:(t + 1) * P],
                                           xp[:, par, u, i, half * H * X1:(half + 1) * H * X1].rearrange("p (h c) -> p h c", c=2 * X1)[:, :, X1:2 * X1],
                                           start=False, stop=u == T - 1 and i == PARTS - 1, skip_group_check=True)
                    if half == 1:
                        mm.then_inc(s["r_mm"], 1)

                def projection(t):
                    three(bX[:, 0:D + HA], lambda k: xTh[:, k, t, :], lambda k: xTl[:, k, t, :],
                          lambda k: Wph[:, k, :], lambda k: Wpl[:, k, :]).then_inc(s["a_xp"], 1)

                def turn(to, g, rows, ready, done):
                    pe.wait_ge(s[ready], (g + 1) * T)
                    for k in range(K):
                        for t in range(T):
                            mm = pe.transpose(to[:, (k * T + t) * P:(k * T + t + 1) * P], rows[:, t, k * P:(k + 1) * P], ident[:, :])
                    mm.then_inc(s[done], 1)

                def mask_turned():
                    pe.wait_ge(s["a_mb"], a + 1)
                    if c is not None and not (isinstance(c, int) and c == 0):
                        pe.wait_ge(s["c_cTs"], c)
                    elif not (isinstance(a, int) and a == 0):
                        pe.wait_ge(s["a_row"], a)
                    for u in range(T):
                        for t in range(T):
                            mm = pe.transpose(bS[:, 0:N].bitcast(BF16)[:, (u * T + t) * P:(u * T + t + 1) * P], mb[:, t, u, :], ident16[:, :])
                    mm.then_inc(s["a_mT"], 1)

                def logits():
                    if a is not None:
                        pe.wait_ge(s["a_mneg"], a + 1)
                    else:
                        pe.wait_ge(s["c_cTs"], c)
                    if isinstance(c, int) and c == 0:
                        pe.wait_ge(s["gate_lo"], 1)
                    pe.wait_ge(s["c_lo"], c + 1)
                    three(bS[0:E, 0:N], lambda k: gateh[:, k, :], lambda k: gatel[:, k, :],
                          lambda k: fTh[:, other, k].rearrange("p t n -> p (t n)"),
                          lambda k: fTl[:, other, k].rearrange("p t n -> p (t n)")).then_inc(s["c_lT"], 1)

                def source_rows():
                    pe.wait_ge(s["a_src"], a + 1)
                    if c is not None:
                        held(pe, "c_lTs", c + 1)
                    else:
                        held(pe, "a_mneg", a + 1)
                    for t in range(T):
                        mm = pe.transpose(bS[0:H, t * P:(t + 1) * P], asrc2[:, par, t, :], ident[:, :])
                    mm.then_inc(s["a_rT"], 1)

                def node_mean():
                    if a is not None:
                        pe.wait_ge(s["a_ev"], (a + 1) * T)
                    for u in range(T):
                        mm = pe.matmul(bX[:, 0:D].rearrange("p (h k) -> p h k", h=H), mean_w[:, :], xh1[:, other, u, :, 0:KH],
                                       start=u == 0, stop=u == T - 1)
                    mm.then_inc(s["b_S"], 1)

                chunk(0)
                chunk(1)
                neighbours(0, 0)
                neighbours(0, 1)
                if a is not None:
                    if c is not None and not (isinstance(c, int) and c == 0):
                        pe.wait_ge(s["c_lo"], c)
                    turn(bT, a, xn, "a_xn", "a_xT")
                chunk(2)
                if a is not None:
                    pe.wait_ge(s["a_lo"], a + 1)
                    if not (isinstance(a, int) and a <= 1):
                        pe.wait_ge(s["b_Sb"], a - 1)
                    projection(0)
                if c is not None:
                    turn(bT, c, xf, "c_xn", "c_xT")
                if a is not None:
                    mask_turned()
                chunk(3)
                if a is not None:
                    pe.wait_ge(s["a_ev"], a * T + 1)
                    projection(1)
                if c is not None:
                    logits()
                neighbours(1, 0)
                if a is not None:
                    source_rows()
                chunk(4)
                neighbours(1, 1)
                if c is not None:
                    if a is not None:
                        held(pe, "a_row", a + 1)
                    held(pe, "c_lTs", c + 1)
                    for t in range(T):
                        mm = pe.transpose(bS[:, t * E:(t + 1) * E], lgT[:, t * P:(t + 1) * P], ident[0:E, 0:E])
                    mm.then_inc(s["c_lb"], 1)
                if b is not None:
                    node_mean()
                chunk(5)
                chunk(6)
                chunk(7)
                if c is not None:
                    held(pe, "c_c3", c + 1)
                    for t in range(T):
                        mm = pe.transpose(bS[0:3 * E, t * P:(t + 1) * P], c3[:, t].rearrange("p a b -> p (a b)"), ident[:, :])
                    mm.then_inc(s["c_cT"], 1)
                chunk(8)
                if isinstance(a, int) and a == 0:
                    v_rows()

            with pe.If(fast_path(pe) == 1):
                iterations(pe, body)
            with pe.Else():
                v_rows()
                pe.wait_ge(s["v_sb"], 1)
                with pe.Fori(0, G) as g:
                    pe.wait_ge(s["xn_d"], (g + 1) * T)
                    for k in range(K):
                        for t in range(T):
                            mm = pe.transpose(pT[:, (k * T + t) * P:(k * T + t + 1) * P], xn[:, t, k * P:(k + 1) * P], ident[:, :])
                    mm.then_inc(s["xT_mm"], 1)
                    pe.wait_ge(s["xTl_d"], g + 1)
                    for t, bk in enumerate((pA, pB)):
                        for k in range(K):
                            for i, (a, b) in enumerate(((xTh, Wph), (xTh, Wpl), (xTl, Wph))):
                                mm = pe.matmul(bk[:, 0:D + HA], a[:, k, t, :], b[:, k, :], start=k == 0 and i == 0, stop=k == K - 1 and i == 2)
                    mm.then_inc(s["xp_mm"], 1)
                    pe.wait_ge(s["adst_d"], (g + 1) * T)
                    pe.wait_ge(s["xh_d"], (g + 1) * T)
                    for n in range(T * H):
                        t, h = n // H, n % H
                        i = g * T * H + n + 1
                        if n:
                            pe.wait_ge(s["vmax_d"], i - 1)
                        for u in range(T):
                            mm = pe.transpose(pC[:, u * P:(u + 1) * P], adst[:, u, h:h + 1].broadcast_to([P, P]), ident[:, :])
                        mm.then_inc(s["bc_mm"], 1)
                        pe.wait_ge(s["prob_d"], i)
                        for u in range(T):
                            mm = pe.transpose(pT[:, u * P:(u + 1) * P], prob[:, u * P:(u + 1) * P], ident[:, :])
                        mm.then_inc(s["pT_mm"], 1)
                        pe.wait_ge(s["pT_d"], i)
                        if n:
                            pe.wait_ge(s["att_d"], i - 1)
                        for u in range(T):
                            mm = pe.matmul(pA[:, 0:KH], probT[:, u, :], xh[:, u, h * KH:(h + 1) * KH], start=u == 0, stop=u == T - 1)
                        mm.then_inc(s["o_mm"], 1)
                with pe.Fori(0, G) as g:
                    pe.wait_ge(s["fxn_d"], (g + 1) * T)
                    for k in range(K):
                        for t in range(T):
                            mm = pe.transpose(pT[:, (k * T + t) * P:(k * T + t + 1) * P], xn[:, t, k * P:(k + 1) * P], ident[:, :])
                    mm.then_inc(s["fxT_mm"], 1)
                    pe.wait_ge(s["fxTl_d"], g + 1)
                    for t in range(T):
                        for k in range(K):
                            for i, (a, b) in enumerate(((xTh, gateh), (xTh, gatel), (xTl, gateh))):
                                mm = pe.matmul(pA[:, t * E:(t + 1) * E], a[:, k, t, :], b[:, k, :], start=k == 0 and i == 0, stop=k == K - 1 and i == 2)
                    mm.then_inc(s["lg_mm"], 1)
                    pe.wait_ge(s["cmb_d"], (g + 1) * T)
                    for t in range(T):
                        mm = pe.transpose(pB[0:E, t * P:(t + 1) * P], cmb[:, t, :], ident[:, :])
                    mm.then_inc(s["cT_mm"], 1)
                    pe.wait_ge(s["cT_d"], g + 1)
                    for t in range(T):
                        mm = pe.matmul(pC[:, t * D:(t + 1) * D], cT[:, t, :], V[:, :], start=True, stop=True)
                    mm.then_inc(s["v_mm"], 1)
                    for b in range(T * E // 2):
                        q, t = b // T, b % T
                        if b >= 4:
                            pe.wait_ge(s["e_acc"], g * T * E + 2 * (b - 3))
                        for k in range(K):
                            for i, (a, w) in enumerate(((xTh, Weh), (xTh, Wel), (xTl, Weh))):
                                mm = pe.matmul(pE[b % 4][:, :], a[:, k, t, :], w[:, k, 2 * q:2 * q + 2, :].rearrange("p e d -> p (e d)"),
                                               start=k == 0 and i == 0, stop=k == K - 1 and i == 2)
                        mm.then_inc(s["e_mm"], 1)


_INS = ["x", "adj", "L0_gnn_W_proj", "L0_gnn_W_att", "L0_gnn_b_att", "L0_ffn_Ins_tk", "L0_ffn_gate_w",
        "L0_ffn_expert_w", "L0_ffn_expert_b", "L0_ffn_gamma_w", "L0_ffn_beta_w", "L0_ffn_rmod_w"]


def kernel(**inputs):
    import concourse.bacc as bacc
    import numpy as np
    from concourse.bass_utils import run_bass_kernel_spmd

    nc = bacc.Bacc("TRN2", target_bir_lowering=False, num_devices=1)
    arrays, args = {}, []
    for name in _INS:
        a = np.asarray(inputs[name])
        a = np.ascontiguousarray(a.T if name == "L0_ffn_gamma_w" else a)
        arrays[f"in_{name}"] = a
        args.append(nc.dram_tensor(f"in_{name}", a.shape, mybir.dt.from_np(a.dtype), kind="ExternalInput").ap())
    out = nc.dram_tensor("out", arrays["in_x"].shape, F32, kind="ExternalOutput").ap()
    program(nc, *args, out)
    result = run_bass_kernel_spmd(nc, [arrays], core_ids=[0])
    return result.results[0]["out"]
```

```python
from contextlib import ExitStack

import concourse.bass as bass
from concourse import mybir

F32 = mybir.dt.float32
F32R = mybir.dt.float32r
BF16 = mybir.dt.bfloat16
I32 = mybir.dt.int32
ALU = mybir.AluOpType
ACT = mybir.ActivationFunctionType
AX = mybir.AxisListType

P = 128
EPS = 1e-5
SLOPE = 0.2
MASKED = -1e30
SENTINEL = -3e38
BOUND = 30.0
AR = 2
RING = 8
PARTS = 3
LAG = 5
FILL = 3


def program(nc, x, adj, W_proj, W_att, b_att, ins_tk, gate_w, expert_w, expert_b, gamma_t, beta_w, rmod_w, out):
    G, N, D = x.shape
    H, two_k = W_att.shape
    KH = two_k // 2
    E = gate_w.shape[1]
    NI = ins_tk.shape[1]
    T = N // P
    K = D // P
    HA = 2 * H
    X1 = KH + 1
    assert T == 2 and K == 2 and H * KH == D and D == N and E == 8 and G % 2 == 0

    row_dram = nc.dram_tensor("row_dram", [2, H * N], F32, kind="Internal").ap()

    with ExitStack() as ctx:
        def sb(name, shape, dt=F32):
            return ctx.enter_context(nc.sbuf_tensor(name, shape, dt))

        def bank(name, n=1):
            return ctx.enter_context(nc.psum_tensor(name, [P, 512] if n == 1 else [P, n, 512], F32))

        def sem(name):
            return ctx.enter_context(nc.semaphore(name))

        x_all = sb("x_all", [P, G, T, D])
        abc = x_all[:, RING:2 * RING].rearrange("p (b g) t d -> p b (g t d)", b=2)
        beta_sb = x_all[:, 3 * RING:4 * RING].rearrange("p (k g) t d -> p k (g t) d", k=K)
        ybuf = x_all[:, 2 * RING:2 * RING + 4]
        tb = x_all[:, 2 * RING + 4:2 * RING + 8].rearrange("p g t d -> p (g t d)").bitcast(BF16).rearrange("p (u h i) -> p u h i", u=T, h=H)
        adj_ring = sb("adj_ring", [P, AR, T, N], I32)

        ident = sb("ident", [P, P])
        ident16 = sb("ident16", [P, P], BF16)
        ones = sb("ones", [P, P])
        mean_w = sb("mean_w", [P, P])
        Wp = sb("Wp", [P, K, D + HA])
        Wph = sb("Wph", [P, K, D + HA], F32R)
        Wpl = sb("Wpl", [P, K, D + HA], F32R)
        Watt = sb("Watt", [P, H, 2, KH])
        batt = sb("batt", [P, H])
        wprod = sb("wprod", [P, H, KH])
        wsq = sb("wsq", [P, K, HA])
        bnd = sb("bnd", [P, 6])
        flag = sb("flag", [P, 1], I32)
        big = sb("big", [P, K, E, D])
        below = big[:, :, :, :].rearrange("p k e d -> p (k e d)").bitcast(BF16).rearrange("p (b u h i) -> p b u h i", b=2, u=T, h=H)
        Weh = sb("Weh", [P, K, E, D], F32R)
        Wel = sb("Wel", [P, K, E, D], F32R)
        gate = sb("gate", [P, K, E])
        gate2 = sb("gate2", [P, K, 2 * E], F32R)
        gateh, gatel = gate2[:, :, 0:E], gate2[:, :, E:2 * E]
        rmod = sb("rmod", [P, K, E])
        gammaT = sb("gammaT", [P, K, E])
        insr = sb("insr", [NI, D])
        ninv = sb("ninv", [NI, 1])
        insm = sb("insm", [P, K])
        gam_all = sb("gam_all", [P, E])
        gam_col = sb("gam_col", [E, 1])
        rgam = sb("rgam", [P, E])
        expb = sb("expb", [E, D])
        eye = sb("eye", [P, E, E])
        insd = sb("insd", [P, K, E, 3, E])
        gamd = sb("gamd", [E, 3, E])
        Vr = sb("Vr", [3 * E, D])
        Vh = sb("Vh", [3 * E, D], F32R)
        Vl = sb("Vl", [3 * E, D])
        V3 = sb("V3", [3 * E, D], F32R)
        rowsel = sb("rowsel", [3 * E, 2])
        V = Vr[0:E, :]

        stats = sb("stats", [P, T, 6])
        mv = sb("mv", [P, T, 2])
        vare = sb("vare", [P, T])
        mhalf = sb("mhalf", [P, T])
        rstd = sb("rstd", [P, T])
        xn = sb("xn", [P, T, D])
        xTh = sb("xTh", [P, K, T, P], F32R)
        xTl = sb("xTl", [P, K, T, P], F32R)
        stats2 = sb("stats2", [P, T, 6])
        mv2 = sb("mv2", [P, T, 2])
        vare2 = sb("vare2", [P, T])
        rstd2 = sb("rstd2", [P, T])
        xf = sb("xf", [P, T, D])
        fTh = sb("fTh", [P, 2, K, T, P], F32R)
        fTl = sb("fTl", [P, 2, K, T, P], F32R)

        xh1 = sb("xh1", [P, 2, T, H, X1])
        ab = sb("ab", [P, 2, T, HA])
        asrc2 = sb("asrc2", [P, 2, T, H])
        beta2 = sb("beta2", [P, T, H, 2])
        rho = sb("rho", [P, 2, T, H])
        mb = sb("mb", [P, T, T, P], BF16)
        mtn = sb("mtn", [P, 2, T, N], BF16)
        thr = sb("thr", [P, T, N], BF16)
        arow = sb("arow", [H, N])
        xe = sb("xe", [P, T, H, 2, X1])
        xp = sb("xp", [P, 2, T, PARTS, H * 2 * X1], BF16)
        xsum = sb("xsum", [P, H, KH])
        sbc = sb("sbc", [P, 2, D])
        nt = sb("nt", [P, T, H, X1])
        nn = sb("nn", [P, T, H, X1])
        emp = sb("emp", [P, T, 1])
        dsum = sb("dsum", [P, T, H])
        rden = sb("rden", [P, T, H])
        oo = sb("oo", [P, T, D])

        spare = xp[:, :, :, :, :].rearrange("p b t c n -> p (b t c n)").bitcast(F32)
        mbias = spare[:, 0:512].rearrange("p (t n) -> p t n", t=T)
        att = spare[:, 512:1024].rearrange("p (t n) -> p t n", t=T)
        vsc, lsc, prob = (spare[:, 1024 + i * 256:1280 + i * 256] for i in range(3))
        probT = spare[:, 1792:2048].rearrange("p (t n) -> p t n", t=T)
        xh = xe[:, :, :, :, :].rearrange("p t h c k -> p (t h c k)")[:, 0:T * D].rearrange("p (t d) -> p t d", t=T)
        asrc, adst = asrc2[:, 0], asrc2[:, 1]
        rmax = sb("rmax", [P, 4])
        psum_row = sb("psum_row", [P, 1])
        rrow = sb("rrow", [P, 1])

        lgT = sb("lgT", [2 * E, N])
        lgs = sb("lgs", [P, T, E])
        lg = sb("lg", [P, T, 16])
        rep = sb("rep", [P, T, 16])
        m8 = sb("m8", [P, T, 8])
        vals = sb("vals", [P, T, 8])
        nmx = sb("nmx", [P, T])
        lgm = sb("lgm", [P, T, E])
        sel = sb("sel", [P, T, E])
        ex = sb("ex", [P, T, E])
        exs = sb("exs", [P, T])
        rex = sb("rex", [P, T])
        exsel = sb("exsel", [P, T, E])
        cmb2 = sb("cmb2", [P, 2, T, E])
        cmb = cmb2[:, 0]
        c3 = sb("c3", [P, T, 3, E])
        cT = sb("cT", [E, T, P])
        cT3 = sb("cT3", [3 * E, 2, T, P], F32R)
        acc2 = sb("acc2", [P, 2, T, D])
        acc = acc2[:, 0]
        yfold = sb("yfold", [P, 2, T, D])

        bT, bX, bS = bank("bT"), bank("bX"), bank("bS")
        bR = bank("bR", 2)
        bE = [bank(f"bE{i}") for i in range(3)]
        pT, pA, pB, pC = bT, bX, bS, bR[:, 0]
        pE = [bR[:, 1], *bE]

        names = """id_zero id_one eye16 consts w_in att_in small_in exp_in beta_in watt_prod watt_sum wp_hi wp_lo
            insm_mm insm_sb mod_mm mod_sb diag gate_hi gate_lo exp_scaled exp_hi exp_lo bet_mm v_raw v_hi v_lo v_sel v_sb
            wsq_d wsq_mm bnd_max bnd_ok flag_d x_in adj_in"""
        fast_names = """a_xn a_xT a_hi a_lo a_xp a_ev a_src a_beta a_mb a_mT a_mneg a_rT a_row
            row_out abc_first abc_second b_q b_thr b_t b_rho b_xe b_p0 b_r b_p1 b_p2 b_sum b_S b_Sb
            r_mm r_t0 r_n r_e r_ds r_rd r_o r_z r_x1
            c_stats c_mv c_var c_rstd c_xn c_xT c_hi c_lo c_lT c_lTs c_lb c_ls c_lg c_m8 c_vals c_lgm c_rep c_sel c_ex c_sum
            c_rec c_es c_cmb c_ch c_cl c_c3 c_cT c_cTs
            d_mm d_dve d_act d_link d_pool f_fin f_out
            a_stats a_mv a_var a_rstd"""
        slow_names = """stats_d mv_d vare_d rstd_d xn_d xT_mm xTh_d xTl_d xp_mm xh_d asrc_d adst_d mask1 mask2
            bc_mm vmax_d top1 top2 t_d l_d prob_d pT_mm pT_d o_mm rrow_d att_d x1_d
            fstats_d fmv_d fvare_d frstd_d fxn_d fxT_mm fxTh_d fxTl_d lg_mm lg_d m8_d vals_d rep_d sel_d nmx_d ex_d
            rex_d cmb_d cT_mm cT_d v_mm base_d e_mm e_acc out_d"""
        s = {n: sem(n) for n in (names + " " + fast_names).split()}
        s.update(zip(slow_names.split(), (s[n] for n in fast_names.split())))
        assert len(slow_names.split()) <= len(fast_names.split())

        def held(eng, name, value, const=("id_one", 2)):
            if isinstance(value, int):
                eng.wait_ge(s[name], value)
            else:
                register = eng.to_reg(value)
                eng.wait_ge(s[const[0]], const[1])
                eng.wait_ge(s[name], register)

        def fast_path(eng):
            eng.wait_ge(s["flag_d"], 1)
            return eng.value_load(flag[0:1, 0:1], min_val=0, max_val=1)

        def iterations(eng, body, end=G):
            def graphs(it):
                return [it - i if 0 <= it - i < G else None for i in range(LAG + 1)]

            for it in range(LAG + 1):
                body(it % 2, *graphs(it))
            with eng.Fori(LAG + 1, end, 2) as it:
                body(0, *(it - i for i in range(LAG + 1)))
                body(1, *(it + 1 - i for i in range(LAG + 1)))
            for it in range(end, G + LAG):
                body(it % 2, *graphs(it))

        def following(a):
            return None if a is None or (isinstance(a, int) and a + 1 == G) else a + 1

        block = ctx.enter_context(nc.Block())

        @block.sync
        def _(sp):
            def load_x(g, slot):
                sp.dma_start(x_all[:, slot], x[g].rearrange("(p t) d -> p t d", t=T)).then_inc(s["x_in"], 16)

            def load_adj(g, slot):
                sp.dma_start(adj_ring[:, slot], adj[g].rearrange("(p t) n -> p t n", t=T)).then_inc(s["adj_in"], 16)

            load_x(0, 0)
            sp.dma_start(Wp[:, :, 0:D], W_proj.rearrange("(k p) o -> p k o", p=P)).then_inc(s["w_in"], 16)
            sp.dma_start(Watt[:, :, :, :].rearrange("p h c k -> p (h c k)"),
                         W_att.rearrange("h k -> (h k)").partition_broadcast(P)).then_inc(s["att_in"], 16)
            sp.dma_start(batt[:, :], b_att.partition_broadcast(P)).then_inc(s["att_in"], 16)
            sp.dma_start(insr[:, :], ins_tk[0]).then_inc(s["small_in"], 16)
            sp.dma_start(gate[:, :, :], gate_w.rearrange("(k p) e -> p k e", p=P)).then_inc(s["small_in"], 16)
            sp.dma_start(rmod[:, :, :], rmod_w.rearrange("(k p) e -> p k e", p=P)).then_inc(s["small_in"], 16)
            sp.dma_start(gammaT[:, :, :], gamma_t.rearrange("(k p) e -> p k e", p=P)).then_inc(s["small_in"], 16)
            sp.dma_start(expb[:, :], expert_b).then_inc(s["small_in"], 16)
            load_adj(0, 0)
            for k in range(K):
                sp.dma_start(big[:, k], expert_w[:, k * P:(k + 1) * P].rearrange("e p d -> p e d")).then_inc(s["exp_in"], 16)
            sp.wait_ge(s["x_in"], 16)
            load_x(1, 1)
            for k in range(K):
                sp.dma_start(beta_sb[:, k], beta_w[:, k * P:(k + 1) * P].rearrange("e p d -> p e d")).then_inc(s["beta_in"], 16)

            def body(par, a, b, r, c, d, f):
                if a is not None and not (isinstance(a, int) and a + 2 >= G):
                    sp.wait_ge(s["x_in"], (a + 2) * 16)
                    load_x(a + 2, (a + 2) % RING)
                if a is not None and not (isinstance(a, int) and a + 1 == G):
                    sp.wait_ge(s["adj_in"], (a + 1) * 16)
                    if not isinstance(a, int) or a >= 1:
                        sp.wait_ge(s["a_mb"], a)
                    load_adj(a + 1, 1 - par)
                if a is not None:
                    sp.wait_ge(s["a_row"], a + 1)
                    sp.dma_start(row_dram[par].rearrange("(h i) -> h i", h=H), arow[:, :]).then_inc(s["row_out"], 16)
                    sp.wait_ge(s["row_out"], (a + 1) * 16)
                    half = H * N // 2
                    sp.dma_start(abc[:, par, 0:half], row_dram[par, 0:half].partition_broadcast(P)).then_inc(s["abc_first"], 16)
                    sp.dma_start(abc[:, par, half:2 * half], row_dram[par, half:2 * half].partition_broadcast(P)).then_inc(s["abc_second"], 16)
                if f is not None:
                    sp.wait_ge(s["f_fin"], f + 1)
                    sp.dma_start(out[f].rearrange("(p t) d -> p t d", t=T), acc2[:, 1 - par]).then_inc(s["f_out"], 16)

            with sp.If(fast_path(sp) == 1):
                iterations(sp, body, G - 4)
                sp.wait_ge(s["f_out"], G * 16)
            with sp.Else():
                sp.sem_inc(s["out_d"], 16)
                sp.wait_ge(s["bet_mm"], 1)
                for first, last in ((1, AR), (AR, G)):
                    with sp.Fori(first, last) as g:
                        if first == AR:
                            sp.wait_ge(s["x_in"], g * 16)
                            load_x(g, g)
                        sp.wait_ge(s["w_in"], 16)
                        sp.wait_ge(s["adj_in"], g * 16)
                        if first == AR:
                            sp.wait_ge(s["mask1"], (g - AR + 1) * T)
                        load_adj(g, g % AR)
                with sp.Fori(0, G) as g:
                    sp.wait_ge(s["e_acc"], (g + 1) * T * E)
                    sp.dma_start(out[g].rearrange("(p t) d -> p t d", t=T), acc[:, :, :]).then_inc(s["out_d"], 16)
                sp.wait_ge(s["out_d"], (G + 1) * 16)

        @block.gpsimd
        def _(pool):
            pool.memset(ident[:, :], 0.0).then_inc(s["id_zero"], 1)
            pool.memset(eye[:, :, :], 0.0).then_inc(s["id_zero"], 1)
            pool.memset(rowsel[:, :], 1.0).then_inc(s["id_zero"], 1)
            pool.memset(ones[:, :], 1.0).then_inc(s["consts"], 1)
            pool.memset(mean_w[:, :], 1.0 / N).then_inc(s["consts"], 1)
            pool.memset(mhalf[:, :], -0.5).then_inc(s["consts"], 1)
            pool.memset(ninv[:, :], 1.0 / NI).then_inc(s["consts"], 1)
            pool.memset(vals[:, :, :], SENTINEL).then_inc(s["consts"], 1)
            pool.memset(lg[:, :, :], SENTINEL).then_inc(s["consts"], 1)
            pool.memset(xh1[:, :, :, :, KH], 1.0).then_inc(s["consts"], 1)
            pool.wait_ge(s["id_zero"], 3)
            pool.affine_select(out=ident[:, :], in_=ident[:, :], compare_op=ALU.not_equal, fill=1.0, base=0,
                               pattern=[[-1, P]], channel_multiplier=1).then_inc(s["id_one"], 1)
            pool.affine_select(out=eye[:, :, :], in_=eye[:, :, :], compare_op=ALU.not_equal, fill=1.0, base=0,
                               pattern=[[1, E], [-1, E]], channel_multiplier=0).then_inc(s["id_one"], 1)
            pool.affine_select(out=rowsel[:, 0:1], in_=rowsel[:, 0:1], compare_op=ALU.is_gt, fill=0.0, base=2 * E,
                               pattern=[[0, 1]], channel_multiplier=-1).then_inc(s["id_one"], 1)
            pool.affine_select(out=rowsel[:, 1:2], in_=rowsel[:, 1:2], compare_op=ALU.is_ge, fill=0.0, base=-2 * E,
                               pattern=[[0, 1]], channel_multiplier=1).then_inc(s["id_one"], 1)
            pool.wait_ge(s["id_one"], 4)
            pool.tensor_copy(ident16[:, :], ident[:, :]).then_inc(s["eye16"], 1)

            def rsqrt(pre, g, m, v, o):
                held(pool, pre + "_mv", (g + 1) * T)
                pool.tensor_scalar(v[:, :], m[:, :, 1], EPS, 1.0, ALU.add, ALU.mult).then_inc(s[pre + "_var"], 1)
                pool.wait_ge(s[pre + "_var"], g + 1)
                pool.tensor_tensor(o[:, :], v[:, :], mhalf[:, :], ALU.pow).then_inc(s[pre + "_rstd"], 1)

            rsqrt("a", 0, mv, vare, rstd)

            def expert_scaled():
                pool.wait_ge(s["exp_in"], 16 * K)
                pool.wait_ge(s["mod_sb"], 3)
                for half in range(2):
                    es = slice(half * E // 2, (half + 1) * E // 2)
                    pool.tensor_tensor(big[:, :, es, :], big[:, :, es, :],
                                       gam_all[:, es].unsqueeze(1).unsqueeze(3).broadcast_to([P, K, E // 2, D]), ALU.mult).then_inc(s["exp_scaled"], 1)

            def fold(t, g, q):
                y = ybuf[:, 2 * t:2 * t + 2]
                pool.wait_ge(s["d_act"], g * 4 + 3 + t)
                pool.tensor_tensor(y[:, 0], y[:, 0], y[:, 1], ALU.add).then_inc(s["d_pool"], 1)
                pool.wait_ge(s["d_pool"], g * 4 + 2 * t + 1)
                pool.tensor_tensor(yfold[:, q, t, :], y[:, 0, 0, :], y[:, 0, 1, :], ALU.add).then_inc(s["d_pool"], 1)

            def body(par, a, b, r, c, d, f):
                other = 1 - par
                xe_t = xe[:, :, :, :, :].rearrange("p t h c k -> p t (h c k)")

                def weighed():
                    pool.wait_ge(s["a_ev"], (b + 1) * T)
                    pool.wait_ge(s["a_beta"], b + 1)
                    if not (isinstance(b, int) and b == 0):
                        pool.wait_ge(s["b_p2"], b)
                    pool.tensor_tensor(xe[:, :, :, :, :].rearrange("p t h c k -> p (t h) c k"),
                                       xh1[:, other].rearrange("p t h k -> p (t h) k").unsqueeze(2).broadcast_to([P, T * H, 2, X1]),
                                       beta2[:, :, :, :].rearrange("p t h c -> p (t h) c").unsqueeze(3).broadcast_to([P, T * H, 2, X1]),
                                       ALU.mult).then_inc(s["b_xe"], 1)

                def quotient(t):
                    pool.wait_ge(s["r_rd"], r * T + t + 1)
                    pool.tensor_tensor(oo[:, t, :].rearrange("p (h k) -> p h k", h=H), nn[:, t, :, 0:KH],
                                       rden[:, t, :].unsqueeze(2).broadcast_to([P, H, KH]), ALU.mult).then_inc(s["r_o"], 1)

                if b is not None:
                    weighed()
                if c is not None:
                    rsqrt("c", c, mv2, vare2, rstd2)
                if f is not None:
                    fold(1, f, other)
                if r is not None:
                    quotient(0)
                if b is not None:
                    pool.wait_ge(s["b_p0"], b + 1)
                    pool.tensor_tensor(xe_t, xe_t, xp[:, other, :, 0, :], ALU.subtract).then_inc(s["b_r"], 1)
                    if not (isinstance(b, int) and b == 0):
                        pool.wait_ge(s["b_S"], b)
                    pool.tensor_tensor(xsum[:, :, :], xh1[:, other, 0, :, 0:KH], xh1[:, other, 1, :, 0:KH], ALU.add).then_inc(s["b_sum"], 1)
                if b is not None:
                    pool.wait_ge(s["b_p1"], b + 1)
                    pool.tensor_tensor(xp[:, other, :, 2, :], xe_t, xp[:, other, :, 1, :], ALU.subtract).then_inc(s["b_p2"], 1)
                if r is not None:
                    quotient(1)
                if d is not None:
                    fold(0, d, par)
                if following(a) is not None:
                    if a is not None:
                        pool.wait_ge(s["a_xn"], (a + 1) * T)
                    rsqrt("a", following(a), mv, vare, rstd)

            with pool.If(fast_path(pool) == 1):
                expert_scaled()
                iterations(pool, body, G - 2)
            with pool.Else():
                expert_scaled()
                with pool.Fori(0, G) as g:
                    mv_done = pool.to_reg((g + 1) * T)
                    pool.wait_ge(s["id_zero"], 2)
                    pool.wait_ge(s["mv_d"], mv_done)
                    pool.tensor_scalar(vare[:, :], mv[:, :, 1], EPS, None, ALU.add).then_inc(s["vare_d"], 1)
                    pool.wait_ge(s["vare_d"], g + 1)
                    pool.tensor_tensor(rstd[:, :], vare[:, :], mhalf[:, :], ALU.pow).then_inc(s["rstd_d"], 1)
                with pool.Fori(0, G) as g:
                    mv_done = pool.to_reg((g + 1) * T)
                    pool.wait_ge(s["id_zero"], 2)
                    pool.wait_ge(s["fmv_d"], mv_done)
                    pool.tensor_scalar(vare[:, :], mv[:, :, 1], EPS, None, ALU.add).then_inc(s["fvare_d"], 1)
                    pool.wait_ge(s["fvare_d"], g + 1)
                    pool.tensor_tensor(rstd[:, :], vare[:, :], mhalf[:, :], ALU.pow).then_inc(s["frstd_d"], 1)

        @block.scalar
        def _(act):
            act.preload_act_table(ACT.Exp)
            act.wait_ge(s["w_in"], 16)
            act.wait_ge(s["watt_sum"], 2 * K)
            act.activation(Wph[:, :, :].rearrange("p k o -> p (k o)"), Wp[:, :, :].rearrange("p k o -> p (k o)"),
                           ACT.Copy).then_inc(s["wp_hi"], 1)

            def expert_upper():
                for half in range(2):
                    es = slice(half * E // 2, (half + 1) * E // 2)
                    act.wait_ge(s["exp_scaled"], half + 1)
                    for k in range(K):
                        ins = act.activation(Weh[:, k, es, :].rearrange("p e d -> p (e d)"),
                                             big[:, k, es, :].rearrange("p e d -> p (e d)"), ACT.Copy)
                    ins.then_inc(s["exp_hi"], 1)

            def body(par, a, b, r, c, d, f):
                other = 1 - par

                def scaled(k, y):
                    if d is None:
                        return
                    q, t = (k - 1) // T, (k - 1) % T
                    act.wait_ge(s["d_mm"], d * 9 + k + 1)
                    act.wait_ge(s["c_cmb"], d + 1)
                    if not (isinstance(d, int) and d == 0):
                        act.wait_ge(s["d_pool"], (d - 1) * 4 + 2 * (t + 1))
                    for i in range(2):
                        ins = act.activation(ybuf[:, y, i, :], bE[k % 3][:, i * D:(i + 1) * D], ACT.Copy,
                                             scale=cmb2[:, par, t, 2 * q + i:2 * q + i + 1])
                    ins.then_inc(s["d_act"], 1)

                def evacuate(t):
                    act.wait_ge(s["a_xp"], a * T + t + 1)
                    act.activation(xh1[:, par, t, :, 0:KH], bX[:, 0:D].rearrange("p (h k) -> p h k", h=H), ACT.Copy)
                    act.activation(ab[:, par, t, :], bX[:, D:D + HA], ACT.Copy).then_inc(s["a_ev"], 1)

                def part(i, ready):
                    act.wait_ge(s[ready], b + 1)
                    act.activation(xp[:, other, :, i, :], xe[:, :, :, :, :].rearrange("p t h c k -> p t (h c k)"),
                                   ACT.Copy).then_inc(s[f"b_p{i}"], 1)

                def crossings(pair):
                    if b is None:
                        return
                    if pair == 0:
                        act.wait_ge(s["abc_first"], (b + 1) * 16)
                    if pair == H // 4:
                        act.wait_ge(s["abc_second"], (b + 1) * 16)
                    if not (isinstance(b, int) and b == 0):
                        act.wait_ge(s["b_q"], (b - 1) * 4 + pair + 1)
                    for h in (2 * pair, 2 * pair + 1):
                        for u in range(T):
                            ins = act.activation(tb[:, u, h, :], abc[:, other, h * N:(h + 1) * N], ACT.Identity,
                                                 bias=ab[:, other, u, H + h:H + h + 1])
                    ins.then_inc(s["b_t"], 1)

                if b is not None:
                    if not (isinstance(b, int) and b < 2):
                        act.wait_ge(s["r_t0"], (b - 1) * T)
                    act.wait_ge(s["a_src"], b + 1)
                    act.activation(rho[:, other].rearrange("p t h -> p (t h)"), asrc2[:, other].rearrange("p t h -> p (t h)"),
                                   ACT.Exp, scale=1.0 - SLOPE).then_inc(s["b_rho"], 1)
                crossings(0)
                if a is not None:
                    act.wait_ge(s["a_xT"], a + 1)
                    act.activation(xTh[:, :, :, :].rearrange("p k t n -> p (k t n)"), bT[:, :], ACT.Copy).then_inc(s["a_hi"], 1)
                if b is not None:
                    part(0, "b_xe")
                scaled(1, 0)
                scaled(2, 2)
                if a is not None:
                    evacuate(0)
                if c is not None:
                    act.wait_ge(s["c_xT"], c + 1)
                    act.activation(fTh[:, other].rearrange("p k t n -> p (k t n)"), bT[:, :], ACT.Copy).then_inc(s["c_hi"], 1)
                crossings(1)
                if a is not None:
                    evacuate(1)
                if b is not None:
                    part(1, "b_r")
                if c is not None:
                    act.wait_ge(s["c_lT"], c + 1)
                    act.activation(lgT[:, :], bS[0:2 * E, 0:N], ACT.Copy).then_inc(s["c_lTs"], 1)
                if a is not None:
                    act.wait_ge(s["a_ev"], (a + 1) * T)
                    act.activation(beta2[:, :, :, 0], ab[:, par, :, H:HA], ACT.Exp)
                    act.activation(beta2[:, :, :, 1], ab[:, par, :, H:HA], ACT.Exp, scale=SLOPE).then_inc(s["a_beta"], 1)
                crossings(2)
                if a is not None:
                    act.wait_ge(s["a_rT"], a + 1)
                    if not (isinstance(a, int) and a == 0):
                        act.wait_ge(s["row_out"], a * 16)
                    act.activation(arow[:, :], bS[0:H, 0:N], ACT.Copy).then_inc(s["a_row"], 1)
                if c is not None:
                    act.wait_ge(s["c_lgm"], c + 1)
                    act.activation(ex[:, :, :].rearrange("p t e -> p (t e)"), lgm[:, :, :].rearrange("p t e -> p (t e)"),
                                   ACT.Exp).then_inc(s["c_ex"], 1)
                if b is not None:
                    act.wait_ge(s["b_S"], b + 1)
                    act.activation(sbc[:, other, :], bX[:, 0:D], ACT.Copy).then_inc(s["b_Sb"], 1)
                crossings(3)
                if a is not None:
                    act.wait_ge(s["a_mT"], a + 1)
                    act.activation(mtn[:, par].rearrange("p u i -> p (u i)"), bS[:, 0:N].bitcast(BF16), ACT.Copy,
                                   scale=-1.0).then_inc(s["a_mneg"], 1)
                scaled(5, 1)
                if c is not None:
                    act.wait_ge(s["c_cT"], c + 1)
                    act.activation(cT3[:, other].rearrange("e t n -> e (t n)"), bS[0:3 * E, 0:N], ACT.Copy).then_inc(s["c_cTs"], 1)
                scaled(8, 3)
                if isinstance(a, int) and a == 0:
                    expert_upper()

            with act.If(fast_path(act) == 1):
                iterations(act, body)
            with act.Else():
                expert_upper()
                with act.Fori(0, G) as g:
                    act.wait_ge(s["xT_mm"], g + 1)
                    act.activation(xTh[:, :, :, :].rearrange("p k t n -> p (k t n)"), pT[:, :], ACT.Copy).then_inc(s["xTh_d"], 1)
                    act.wait_ge(s["xp_mm"], (g + 1))
                    for t, bk in enumerate((pA, pB)):
                        act.activation(xh[:, t, :], bk[:, 0:D], ACT.Copy).then_inc(s["xh_d"], 1)
                    for n in range(T * H):
                        act.wait_ge(s["l_d"], g * T * H + n + 1)
                        act.activation(prob[:, :], lsc[:, :], ACT.Exp, bias=rmax[:, 3:4], accum_out=psum_row[:, :]).then_inc(s["prob_d"], 1)
                        act.wait_ge(s["pT_mm"], g * T * H + n + 1)
                        act.activation(probT[:, :, :].rearrange("p t n -> p (t n)"), pT[:, 0:N], ACT.Copy).then_inc(s["pT_d"], 1)
                with act.Fori(0, G) as g:
                    act.wait_ge(s["fxT_mm"], g + 1)
                    act.activation(xTh[:, :, :, :].rearrange("p k t n -> p (k t n)"), pT[:, :], ACT.Copy).then_inc(s["fxTh_d"], 1)
                    for t in range(T):
                        act.wait_ge(s["nmx_d"], g * T + t + 1)
                        act.activation(ex[:, t, :], lg[:, t, 0:E], ACT.Exp, bias=nmx[:, t:t + 1], accum_out=exs[:, t:t + 1]).then_inc(s["ex_d"], 1)
                    act.wait_ge(s["cT_mm"], g + 1)
                    act.activation(cT[:, :, :].rearrange("e t n -> e (t n)"), pB[0:E, 0:N], ACT.Copy).then_inc(s["cT_d"], 1)

        @block.vector
        def _(dve):
            def moments(t, g, ready, rows, st, pre):
                held(dve, ready, rows)
                dve.bn_stats(st[:, t, :], x_all[:, g % RING, t, :]).then_inc(s[pre + "_stats"], 1)

            def mean_variance(g, st, m, pre):
                held(dve, pre + "_stats", (g + 1) * T)
                for t in range(T):
                    dve.bn_aggr(m[:, t, :], st[:, t, :]).then_inc(s[pre + "_mv"], 1)

            for t in range(T):
                moments(t, 0, "x_in", 16, stats, "a")
            mean_variance(0, stats, mv, "a")
            dve.wait_ge(s["w_in"], 16)
            dve.wait_ge(s["att_in"], 32)
            n = 0
            for k in range(K):
                for c in range(2):
                    if n:
                        dve.wait_ge(s["watt_sum"], n)
                    dve.tensor_tensor(wprod[:, :, :], Wp[:, k, 0:D].rearrange("p (h k) -> p h k", h=H), Watt[:, :, c, :],
                                      ALU.mult).then_inc(s["watt_prod"], 1)
                    n += 1
                    dve.wait_ge(s["watt_prod"], n)
                    dve.tensor_reduce(Wp[:, k, D + c * H:D + (c + 1) * H], wprod[:, :, :], AX.X, ALU.add).then_inc(s["watt_sum"], 1)
            dve.wait_ge(s["watt_sum"], n)
            dve.tensor_tensor(wsq[:, :, :], Wp[:, :, D:D + HA], Wp[:, :, D:D + HA], ALU.mult).then_inc(s["wsq_d"], 1)
            dve.wait_ge(s["wp_hi"], 1)
            dve.tensor_tensor(Wpl[:, :, :], Wp[:, :, :], Wph[:, :, :].bitcast(F32), ALU.subtract).then_inc(s["wp_lo"], 1)
            dve.wait_ge(s["wsq_mm"], 1)
            dve.tensor_reduce(bnd[:, 0:1], bX[:, 0:HA], AX.X, ALU.max).then_inc(s["bnd_max"], 1)
            dve.tensor_reduce(bnd[:, 1:2], batt[:, :], AX.X, ALU.max, apply_absolute_value=True).then_inc(s["bnd_max"], 1)
            dve.wait_ge(s["bnd_max"], 2)
            dve.tensor_scalar(bnd[:, 2:3], bnd[:, 0:1], BOUND * BOUND / D, None, ALU.is_le).then_inc(s["bnd_ok"], 1)
            dve.tensor_scalar(bnd[:, 3:4], bnd[:, 1:2], BOUND, None, ALU.is_le).then_inc(s["bnd_ok"], 1)
            dve.wait_ge(s["insm_mm"], 1)
            dve.tensor_copy(insm[:, :], bS[:, 0:K]).then_inc(s["insm_sb"], 1)
            dve.wait_ge(s["bnd_ok"], 2)
            dve.tensor_tensor(flag[:, :], bnd[:, 2:3], bnd[:, 3:4], ALU.mult).then_inc(s["flag_d"], 1)

            dve.wait_ge(s["small_in"], 16 * 5)
            dve.tensor_copy(gateh[:, :, :], gate[:, :, :]).then_inc(s["gate_hi"], 1)
            dve.wait_ge(s["gate_hi"], 1)
            dve.tensor_tensor(gatel[:, :, :], gate[:, :, :], gateh[:, :, :].bitcast(F32), ALU.subtract).then_inc(s["gate_lo"], 1)
            def modulation():
                dve.wait_ge(s["mod_mm"], 1)
                dve.tensor_copy(gam_all[:, :], bS[:, 16:16 + E]).then_inc(s["mod_sb"], 1)
                dve.tensor_copy(rgam[:, :], bS[:, 32:32 + E]).then_inc(s["mod_sb"], 1)
                dve.tensor_copy(gam_col[:, :], bS[0:E, 48:49]).then_inc(s["mod_sb"], 1)
                dve.wait_ge(s["mod_sb"], 3)
                dve.wait_ge(s["id_one"], 4)
                for k in range(K):
                    dve.tensor_scalar(insd[:, k], eye[:, :, :].unsqueeze(2).broadcast_to([P, E, 3, E]), insm[:, k:k + 1], None,
                                      ALU.mult).then_inc(s["diag"], 1)
                dve.tensor_scalar(gamd[:, :, :], ident[0:E, 0:E].unsqueeze(1).broadcast_to([E, 3, E]), gam_col[:, 0:1], None,
                                  ALU.mult).then_inc(s["diag"], 1)

            def expert_lower(half):
                es = slice(half * E // 2, (half + 1) * E // 2)
                dve.wait_ge(s["exp_hi"], half + 1)
                dve.tensor_tensor(Wel[:, :, es, :], big[:, :, es, :], Weh[:, :, es, :].bitcast(F32), ALU.subtract).then_inc(s["exp_lo"], 1)

            def v_rows():
                dve.wait_ge(s["bet_mm"], 1)
                dve.tensor_copy(Vr[:, :], bE[0][0:3 * E, 0:D]).then_inc(s["v_raw"], 1)
                dve.wait_ge(s["v_raw"], 1)
                dve.tensor_copy(Vh[:, :], Vr[:, :]).then_inc(s["v_hi"], 1)
                dve.wait_ge(s["v_hi"], 1)
                dve.tensor_tensor(Vl[:, :], Vr[:, :], Vh[:, :].bitcast(F32), ALU.subtract).then_inc(s["v_lo"], 1)
                dve.wait_ge(s["v_lo"], 1)
                dve.tensor_scalar(Vl[:, :], Vl[:, :], rowsel[:, 1:2], None, ALU.mult).then_inc(s["v_sel"], 1)
                dve.wait_ge(s["v_sel"], 1)
                dve.scalar_tensor_tensor(V3[:, :], Vh[:, :].bitcast(F32), rowsel[:, 0:1], Vl[:, :], ALU.mult, ALU.add).then_inc(s["v_sb"], 1)

            def body(par, a, b, r, c, d, f):
                other = 1 - par

                def targets(pair):
                    if b is None:
                        return
                    if isinstance(b, int) and b == 0 and pair == 0:
                        dve.wait_ge(s["exp_lo"], 2)
                    dve.wait_ge(s["b_t"], b * 4 + pair + 1)
                    dve.wait_ge(s["b_thr"], b + 1)
                    dve.tensor_tensor(below[:, other, :, 2 * pair:2 * pair + 2, :], tb[:, :, 2 * pair:2 * pair + 2, :],
                                      thr[:, :, :].unsqueeze(2).broadcast_to([P, T, 2, N]), ALU.is_le).then_inc(s["b_q"], 1)

                def expert(k, half, number, before):
                    if d is None:
                        return
                    q, t = (k - 1) // T, (k - 1) % T
                    if half == 0:
                        dve.wait_ge(s["d_mm"], d * 9 + k + 1)
                        dve.wait_ge(s["d_dve"], d * 5 + before)
                    else:
                        dve.wait_ge(s["d_link"], d * 4 + number - 1)
                    dve.scalar_tensor_tensor(acc2[:, par, t, :], bE[k % 3][:, half * D:(half + 1) * D],
                                             cmb2[:, par, t, 2 * q + half:2 * q + half + 1], acc2[:, par, t, :], ALU.mult,
                                             ALU.add).then_inc(s["d_dve" if half else "d_link"], 1)

                sums = bR[:, :, 0:H * X1].rearrange("p f (h c) -> p f h c", c=2 * X1)

                def scaled_sums(t):
                    if r is None:
                        return
                    dve.wait_ge(s["r_mm"], r * T + t + 1)
                    dve.wait_ge(s["b_rho"], r + 1)
                    dve.tensor_tensor(nt[:, t].rearrange("p (f h) k -> p f h k", f=2), sums[:, :, :, 0:X1],
                                      rho[:, par, t, :].rearrange("p (f h) -> p f h", f=2).unsqueeze(3).broadcast_to([P, 2, H // 2, X1]),
                                      ALU.mult).then_inc(s["r_t0"], 1)

                def row_sums(t):
                    if r is None:
                        return
                    dve.wait_ge(s["r_t0"], r * T + t + 1)
                    dve.tensor_tensor(nn[:, t].rearrange("p (f h) k -> p f h k", f=2), sums[:, :, :, X1:2 * X1],
                                      nt[:, t].rearrange("p (f h) k -> p f h k", f=2), ALU.subtract).then_inc(s["r_n"], 1)

                def empty_rows(t):
                    if r is None:
                        return
                    dve.wait_ge(s["r_n"], r * T + t + 1)
                    dve.tensor_scalar(emp[:, t, :], nn[:, t, 0, KH:X1], 0.0, None, ALU.is_equal).then_inc(s["r_e"], 1)

                def denominators(t):
                    if r is None:
                        return
                    dve.wait_ge(s["r_e"], r * T + t + 1)
                    dve.tensor_scalar(dsum[:, t, :], nn[:, t, :, KH], emp[:, t, :], None, ALU.add).then_inc(s["r_ds"], 1)

                def row_weights(t):
                    if r is None:
                        return
                    dve.wait_ge(s["r_ds"], r * T + t + 1)
                    dve.reciprocal(rden[:, t, :], dsum[:, t, :]).then_inc(s["r_rd"], 1)

                def with_mean(t):
                    if r is None:
                        return
                    dve.wait_ge(s["r_o"], r * T + t + 1)
                    dve.wait_ge(s["b_Sb"], r + 1)
                    dve.scalar_tensor_tensor(oo[:, t, :], sbc[:, par, :], emp[:, t, :], oo[:, t, :], ALU.mult, ALU.add).then_inc(s["r_z"], 1)

                def row_out(t):
                    if r is None:
                        return
                    dve.wait_ge(s["r_z"], r * T + t + 1)
                    dve.scalar_tensor_tensor(x_all[:, r % RING, t, :], oo[:, t, :], 0.0, x_all[:, r % RING, t, :], ALU.max,
                                             ALU.add).then_inc(s["r_x1"], 1)

                def normalise(t, g, to, m, rs, pre):
                    if g is None:
                        return
                    if t == 0:
                        dve.wait_ge(s[pre + "_rstd"], g + 1)
                    dve.tensor_scalar(to[:, t, :], x_all[:, g % RING, t, :], m[:, t, 0:1], rs[:, t:t + 1], ALU.subtract,
                                      ALU.mult).then_inc(s[pre + "_xn"], 1)

                def lower(g, hi, lo, pre):
                    dve.wait_ge(s[pre + "_hi"], g + 1)
                    dve.tensor_tensor(lo.rearrange("p k t n -> p (k t n)"), bT[:, :],
                                      hi.rearrange("p k t n -> p (k t n)").bitcast(F32), ALU.subtract).then_inc(s[pre + "_lo"], 1)

                def neighbour_mask():
                    dve.wait_ge(s["adj_in"], (a + 1) * 16)
                    for t in range(T):
                        ins = dve.tensor_scalar(mb[:, t], adj_ring[:, par, t, :].rearrange("p (q u) -> p u q", u=T), 0, None, ALU.is_gt)
                    ins.then_inc(s["a_mb"], 1)

                def source_terms():
                    dve.wait_ge(s["a_ev"], (a + 1) * T)
                    dve.tensor_tensor(asrc2[:, par], ab[:, par, :, 0:H], batt[:, :].unsqueeze(1).broadcast_to([P, T, H]),
                                      ALU.add).then_inc(s["a_src"], 1)

                def base():
                    dve.wait_ge(s["d_mm"], d * 9 + 1)
                    if not (isinstance(d, int) and d <= 1):
                        dve.wait_ge(s["f_out"], (d - 1) * 16)
                    dve.tensor_tensor(acc2[:, par], bE[0][:, :].rearrange("p (t d) -> p t d", t=T), x_all[:, d % RING],
                                      ALU.add).then_inc(s["d_dve"], 1)

                both = bS[:, 0:2 * T * E].rearrange("p (t c e) -> p t c e", t=T, c=2)

                def router_lower():
                    if c is None:
                        return
                    dve.wait_ge(s["c_lb"], c + 1)
                    dve.tensor_tensor(lgs[:, :, :], both[:, :, 1, :], rgam[:, :].unsqueeze(1).broadcast_to([P, T, E]),
                                      ALU.add).then_inc(s["c_ls"], 1)

                def router_logits():
                    if c is None:
                        return
                    dve.wait_ge(s["c_ls"], c + 1)
                    dve.tensor_tensor(lg[:, :, 0:E], both[:, :, 0, :], lgs[:, :, :], ALU.add).then_inc(s["c_lg"], 1)

                def best():
                    if c is None:
                        return
                    held(dve, "c_lg", c + 1)
                    for t in range(T):
                        dve.max(m8[:, t, :], lg[:, t, 0:E]).then_inc(s["c_m8"], 1)

                def shifted():
                    if c is None:
                        return
                    dve.wait_ge(s["c_m8"], (c + 1) * T)
                    dve.tensor_tensor(lgm[:, :, :], lg[:, :, 0:E], m8[:, :, 0:1].broadcast_to([P, T, E]), ALU.subtract).then_inc(s["c_lgm"], 1)
                    dve.tensor_copy(vals[:, :, 0:2], m8[:, :, 0:2]).then_inc(s["c_vals"], 1)

                def without_best():
                    if c is None:
                        return
                    held(dve, "c_vals", c + 1)
                    for t in range(T):
                        dve.match_replace(rep[:, t, 0:14], vals[:, t, :], lg[:, t, 0:14], SENTINEL).then_inc(s["c_rep"], 1)

                def selection():
                    if c is None:
                        return
                    dve.wait_ge(s["c_rep"], (c + 1) * T)
                    dve.tensor_tensor(sel[:, :, :], rep[:, :, 0:E], lg[:, :, 0:E], ALU.not_equal).then_inc(s["c_sel"], 1)
                    dve.wait_ge(s["c_ex"], c + 1)
                    dve.tensor_reduce(exs[:, :], ex[:, :, :], AX.X, ALU.add).then_inc(s["c_sum"], 1)
                    dve.wait_ge(s["c_sel"], c + 1)
                    dve.tensor_tensor(exsel[:, :, :], ex[:, :, :], sel[:, :, :], ALU.mult).then_inc(s["c_es"], 1)

                def over_sum():
                    if c is None:
                        return
                    dve.wait_ge(s["c_sum"], c + 1)
                    dve.reciprocal(rex[:, :], exs[:, :]).then_inc(s["c_rec"], 1)

                def combine():
                    if c is None:
                        return
                    dve.wait_ge(s["c_es"], c + 1)
                    dve.wait_ge(s["c_rec"], c + 1)
                    dve.tensor_tensor(cmb2[:, other], exsel[:, :, :], rex[:, :].unsqueeze(2).broadcast_to([P, T, E]),
                                      ALU.mult).then_inc(s["c_cmb"], 1)

                def weights_upper():
                    if c is None:
                        return
                    dve.wait_ge(s["c_cmb"], c + 1)
                    dve.tensor_copy(c3[:, :, 0, :].bitcast(F32R), cmb2[:, other]).then_inc(s["c_ch"], 1)

                def weights_lower():
                    if c is None:
                        return
                    dve.wait_ge(s["c_ch"], c + 1)
                    dve.tensor_tensor(c3[:, :, 1, :], cmb2[:, other], c3[:, :, 0, :], ALU.subtract).then_inc(s["c_cl"], 1)
                    dve.tensor_copy(c3[:, :, 2, :], c3[:, :, 0, :]).then_inc(s["c_c3"], 1)

                if b is not None:
                    dve.wait_ge(s["a_mneg"], b + 1)
                    if not (isinstance(b, int) and b == 0):
                        dve.wait_ge(s["b_q"], b * 4)
                    dve.tensor_scalar(thr[:, :, :], mtn[:, other], 1.0, SENTINEL, ALU.add, ALU.mult).then_inc(s["b_thr"], 1)
                for t in range(T):
                    normalise(t, a, xn, mv, rstd, "a")
                if c is not None:
                    for t in range(T):
                        moments(t, c, "r_x1", (c + 1) * T, stats2, "c")
                if a is not None:
                    neighbour_mask()
                if isinstance(a, int) and a == 0:
                    modulation()
                if c is not None:
                    mean_variance(c, stats2, mv2, "c")
                if d is not None:
                    base()
                scaled_sums(0)
                if a is not None:
                    lower(a, xTh[:, :, :, :], xTl[:, :, :, :], "a")
                normalise(0, c, xf, mv2, rstd2, "c")
                row_sums(0)
                normalise(1, c, xf, mv2, rstd2, "c")
                empty_rows(0)
                if isinstance(a, int) and a == 1:
                    expert_lower(0)
                    expert_lower(1)
                targets(0)
                denominators(0)
                row_weights(0)
                if f is not None:
                    dve.wait_ge(s["d_pool"], (f + 1) * 4)
                    dve.wait_ge(s["d_dve"], (f + 1) * 5)
                    dve.tensor_tensor(acc2[:, other], acc2[:, other], yfold[:, other], ALU.add).then_inc(s["f_fin"], 1)
                if c is not None:
                    lower(c, fTh[:, other], fTl[:, other], "c")
                with_mean(0)
                expert(3, 0, 2, 1)
                row_out(0)
                expert(3, 1, 2, 1)
                targets(1)
                if a is not None:
                    source_terms()
                router_lower()
                expert(4, 0, 3, 1)
                router_logits()
                expert(4, 1, 3, 1)
                best()
                shifted()
                scaled_sums(1)
                without_best()
                row_sums(1)
                selection()
                empty_rows(1)
                over_sum()
                denominators(1)
                combine()
                targets(2)
                row_weights(1)
                if following(a) is not None:
                    if a is not None:
                        held(dve, "a_xn", (a + 1) * T)
                    moments(0, following(a), "x_in", (following(a) + 1) * 16, stats, "a")
                weights_upper()
                if following(a) is not None:
                    moments(1, following(a), "x_in", (following(a) + 1) * 16, stats, "a")
                weights_lower()
                with_mean(1)
                expert(6, 0, 4, 3)
                row_out(1)
                targets(3)
                if following(a) is not None:
                    mean_variance(following(a), stats, mv, "a")
                expert(6, 1, 4, 3)
                expert(7, 0, 5, 2)
                expert(7, 1, 5, 2)
                if isinstance(a, int) and a == FILL - 1:
                    v_rows()

            with dve.If(fast_path(dve) == 1):
                iterations(dve, body, G - 2)
            with dve.Else():
                modulation()
                expert_lower(0)
                expert_lower(1)
                v_rows()
                with dve.Fori(0, G) as g:
                    dve.wait_ge(s["x_in"], (g + 1) * 16)
                    for t in range(T):
                        dve.bn_stats(stats[:, t, :], x_all[:, g, t, :]).then_inc(s["stats_d"], 1)
                    for t in range(T):
                        stats_done = dve.to_reg(g * T + t + 1)
                        dve.wait_ge(s["id_one"], 2)
                        dve.wait_ge(s["stats_d"], stats_done)
                        dve.bn_aggr(mv[:, t, :], stats[:, t, :]).then_inc(s["mv_d"], 1)
                    dve.wait_ge(s["rstd_d"], g + 1)
                    for t in range(T):
                        dve.tensor_scalar(xn[:, t, :], x_all[:, g, t, :], mv[:, t, 0:1], rstd[:, t:t + 1], ALU.subtract,
                                          ALU.mult).then_inc(s["xn_d"], 1)
                    dve.wait_ge(s["xTh_d"], g + 1)
                    dve.tensor_tensor(xTl[:, :, :, :].rearrange("p k t n -> p (k t n)"), pT[:, :],
                                      xTh[:, :, :, :].rearrange("p k t n -> p (k t n)").bitcast(F32), ALU.subtract).then_inc(s["xTl_d"], 1)
                    dve.wait_ge(s["xh_d"], (g + 1) * T)
                    for t, bk in enumerate((pA, pB)):
                        dve.tensor_tensor(asrc[:, t, :], bk[:, D:D + H], batt[:, :], ALU.add).then_inc(s["asrc_d"], 1)
                        dve.tensor_copy(adst[:, t, :], bk[:, D + H:D + HA]).then_inc(s["adst_d"], 1)
                    dve.wait_ge(s["adj_in"], (g + 1) * 16)
                    for t in range(T):
                        dve.tensor_scalar(mbias[:, t, :].rearrange("p (u q) -> p u q", u=T),
                                          adj_ring[:, g % AR, t, :].rearrange("p (q u) -> p u q", u=T), 0, None, ALU.is_gt).then_inc(s["mask1"], 1)
                    dve.wait_ge(s["mask1"], (g + 1) * T)
                    dve.tensor_scalar(mbias[:, :, :], mbias[:, :, :], -MASKED, MASKED, ALU.mult, ALU.add).then_inc(s["mask2"], 1)
                    dve.wait_ge(s["mask2"], g + 1)
                    dve.wait_ge(s["asrc_d"], (g + 1) * T)
                    for n in range(T * H):
                        t, h = n // H, n % H
                        i = dve.to_reg(g * T * H + n + 1)
                        dve.wait_ge(s["id_one"], 2)
                        dve.wait_ge(s["bc_mm"], i)
                        dve.tensor_tensor_reduce(vsc[:, :], pC[:, 0:N], mbias[:, t, :], 1.0, -3e38, ALU.add, ALU.max,
                                                 rmax[:, 0:1]).then_inc(s["vmax_d"], 1)
                        dve.wait_ge(s["vmax_d"], i)
                        dve.tensor_scalar(rmax[:, 1:2], rmax[:, 0:1], asrc[:, t, h:h + 1], None, ALU.add).then_inc(s["top1"], 1)
                        dve.tensor_scalar(vsc[:, :], vsc[:, :], asrc[:, t, h:h + 1], None, ALU.add).then_inc(s["t_d"], 1)
                        dve.wait_ge(s["top1"], i)
                        dve.scalar_tensor_tensor(rmax[:, 2:3], rmax[:, 1:2], SLOPE, rmax[:, 1:2], ALU.mult, ALU.max).then_inc(s["top2"], 1)
                        dve.wait_ge(s["t_d"], i)
                        dve.scalar_tensor_tensor(lsc[:, :], vsc[:, :], SLOPE, vsc[:, :], ALU.mult, ALU.max)
                        dve.wait_ge(s["top2"], i)
                        dve.tensor_scalar(rmax[:, 3:4], rmax[:, 2:3], -1.0, None, ALU.mult).then_inc(s["l_d"], 1)
                        dve.wait_ge(s["prob_d"], i)
                        dve.reciprocal(rrow[:, :], psum_row[:, :]).then_inc(s["rrow_d"], 1)
                        dve.wait_ge(s["rrow_d"], i)
                        dve.wait_ge(s["o_mm"], i)
                        dve.tensor_scalar(att[:, t, h * KH:(h + 1) * KH], pA[:, 0:KH], rrow[:, :], None, ALU.mult).then_inc(s["att_d"], 1)
                    dve.wait_ge(s["att_d"], (g + 1) * T * H)
                    dve.scalar_tensor_tensor(x_all[:, g], att[:, :, :], 0.0, x_all[:, g], ALU.max, ALU.add).then_inc(s["x1_d"], 1)

                with dve.Fori(0, G) as g:
                    dve.wait_ge(s["x1_d"], g + 1)
                    for t in range(T):
                        dve.bn_stats(stats[:, t, :], x_all[:, g, t, :]).then_inc(s["fstats_d"], 1)
                    for t in range(T):
                        stats_done = dve.to_reg(g * T + t + 1)
                        dve.wait_ge(s["id_one"], 2)
                        dve.wait_ge(s["fstats_d"], stats_done)
                        dve.bn_aggr(mv[:, t, :], stats[:, t, :]).then_inc(s["fmv_d"], 1)
                    dve.wait_ge(s["frstd_d"], g + 1)
                    for t in range(T):
                        dve.tensor_scalar(xn[:, t, :], x_all[:, g, t, :], mv[:, t, 0:1], rstd[:, t:t + 1], ALU.subtract,
                                          ALU.mult).then_inc(s["fxn_d"], 1)
                    dve.wait_ge(s["fxTh_d"], g + 1)
                    dve.tensor_tensor(xTl[:, :, :, :].rearrange("p k t n -> p (k t n)"), pT[:, :],
                                      xTh[:, :, :, :].rearrange("p k t n -> p (k t n)").bitcast(F32), ALU.subtract).then_inc(s["fxTl_d"], 1)
                    dve.wait_ge(s["lg_mm"], g + 1)
                    dve.wait_ge(s["consts"], 7)
                    for t in range(T):
                        dve.tensor_tensor(lg[:, t, 0:E], pA[:, t * E:(t + 1) * E], rgam[:, :], ALU.add).then_inc(s["lg_d"], 1)
                    for t in range(T):
                        i = dve.snap(g * T + t + 1)
                        dve.wait_ge(s["id_one"], 2)
                        dve.wait_ge(s["lg_d"], i)
                        dve.max(m8[:, t, :], lg[:, t, 0:E]).then_inc(s["m8_d"], 1)
                        dve.wait_ge(s["m8_d"], i)
                        dve.tensor_scalar(nmx[:, t:t + 1], m8[:, t, 0:1], -1.0, None, ALU.mult).then_inc(s["nmx_d"], 1)
                        dve.tensor_copy(vals[:, t, 0:2], m8[:, t, 0:2]).then_inc(s["vals_d"], 1)
                        dve.wait_ge(s["id_one"], 2)
                        dve.wait_ge(s["vals_d"], i)
                        dve.match_replace(rep[:, t, 0:14], vals[:, t, :], lg[:, t, 0:14], SENTINEL).then_inc(s["rep_d"], 1)
                        dve.wait_ge(s["rep_d"], i)
                        dve.tensor_tensor(sel[:, t, :], rep[:, t, 0:E], lg[:, t, 0:E], ALU.not_equal).then_inc(s["sel_d"], 1)
                        dve.wait_ge(s["ex_d"], i)
                        dve.reciprocal(rex[:, t:t + 1], exs[:, t:t + 1]).then_inc(s["rex_d"], 1)
                        dve.wait_ge(s["rex_d"], i)
                        dve.wait_ge(s["sel_d"], i)
                        dve.scalar_tensor_tensor(cmb[:, t, :], ex[:, t, :], rex[:, t:t + 1], sel[:, t, :], ALU.mult, ALU.mult).then_inc(s["cmb_d"], 1)
                    dve.wait_ge(s["v_mm"], g + 1)
                    dve.wait_ge(s["out_d"], (g + 1) * 16)
                    dve.tensor_tensor(acc[:, :, :], pC[:, :].rearrange("p (t d) -> p t d", t=T), x_all[:, g], ALU.add).then_inc(s["base_d"], 1)
                    dve.wait_ge(s["base_d"], g + 1)
                    dve.wait_ge(s["cmb_d"], (g + 1) * T)
                    for n in range(T * E):
                        e, t = n // (2 * T) * 2 + n % 2, n // 2 % T
                        b = n // 2
                        dve.wait_ge(s["e_mm"], g * T * E // 2 + b + 1)
                        if n:
                            dve.wait_ge(s["e_acc"], g * T * E + n)
                        dve.scalar_tensor_tensor(acc[:, t, :], pE[b % 4][:, (n % 2) * D:(n % 2 + 1) * D], cmb[:, t, e:e + 1],
                                                 acc[:, t, :], ALU.mult, ALU.add).then_inc(s["e_acc"], 1)

        @block.tensor
        def _(pe):
            pe.wait_ge(s["consts"], 7)
            pe.wait_ge(s["id_one"], 4)
            pe.wait_ge(s["eye16"], 1)
            pe.wait_ge(s["wsq_d"], 1)
            for k in range(K):
                mm = pe.matmul(bX[:, 0:HA], ones[:, :], wsq[:, k, :], start=k == 0, stop=k == K - 1)
            mm.then_inc(s["wsq_mm"], 1)
            pe.wait_ge(s["small_in"], 16 * 5)
            for k in range(K):
                mm = pe.matmul(bS[:, k:k + 1], insr[:, k * P:(k + 1) * P], ninv[:, :], start=True, stop=True)
            mm.then_inc(s["insm_mm"], 1)
            pe.wait_ge(s["insm_sb"], 1)
            for k in range(K):
                pe.matmul(bS[:, 16:16 + E], insm[:, k:k + 1].broadcast_to([P, P]), gammaT[:, k, :], start=k == 0, stop=k == K - 1)
            for k in range(K):
                pe.matmul(bS[:, 32:32 + E], insm[:, k:k + 1].broadcast_to([P, P]), rmod[:, k, :], start=k == 0, stop=k == K - 1)
            for k in range(K):
                mm = pe.matmul(bS[0:E, 48:49], gammaT[:, k, :], insm[:, k:k + 1], start=k == 0, stop=k == K - 1)
            mm.then_inc(s["mod_mm"], 1)
            pe.wait_ge(s["wp_lo"], 1)
            pe.wait_ge(s["flag_d"], 1)

            def v_rows(piece):
                if piece == 0:
                    pe.wait_ge(s["beta_in"], 16 * K)
                    pe.wait_ge(s["diag"], K + 1)
                for e in range(piece * E // FILL, (piece + 1) * E // FILL):
                    for k in range(K):
                        pe.matmul(bE[0][0:3 * E, 0:D], insd[:, k, e].rearrange("p a b -> p (a b)"), beta_sb[:, k, e, :],
                                  start=e + k == 0, stop=False)
                if piece == FILL - 1:
                    pe.matmul(bE[0][0:3 * E, 0:D], gamd[:, :, :].rearrange("p a b -> p (a b)"), expb[:, :], start=False,
                              stop=True).then_inc(s["bet_mm"], 1)

            def body(par, a, b, r, c, d, f):
                other = 1 - par

                def three(out, hi, lo, whi, wlo, first=True, last=True):
                    for k in range(K):
                        for i, (p, w) in enumerate(((hi, whi), (hi, wlo), (lo, whi))):
                            mm = pe.matmul(out, p(k), w(k), start=k == 0 and i == 0, stop=k == K - 1 and i == 2)
                    return mm

                def chunk(k):
                    if d is None:
                        return
                    freed = {0: ("d_dve", 4, 1), 1: ("d_dve", 5, 1), 2: ("d_act", 4, 1), 3: ("d_dve", 1, 0),
                             4: ("d_act", 1, 0), 5: ("d_act", 2, 0), 6: ("d_dve", 2, 0), 7: ("d_dve", 3, 0), 8: ("d_act", 3, 0)}
                    name, count, back = freed[k]
                    if not (back and isinstance(d, int) and d == 0):
                        pe.wait_ge(s[name], (d - back) * (5 if name == "d_dve" else 4) + count)
                    if k == 0:
                        if isinstance(d, int) and d == 0:
                            pe.wait_ge(s["v_sb"], 1)
                            pe.wait_ge(s["exp_lo"], 2)
                        held(pe, "c_cTs", d + 1)
                        for t in range(T):
                            mm = pe.matmul(bE[0][:, t * D:(t + 1) * D], cT3[:, par, t, :], V3[:, :], start=True, stop=True)
                    else:
                        q, t = (k - 1) // T, (k - 1) % T
                        if k == 1:
                            pe.wait_ge(s["c_lo"], d + 1)
                        mm = three(bE[k % 3][:, :], lambda j: fTh[:, par, j, t, :], lambda j: fTl[:, par, j, t, :],
                                   lambda j: Weh[:, j, 2 * q:2 * q + 2, :].rearrange("p e d -> p (e d)"),
                                   lambda j: Wel[:, j, 2 * q:2 * q + 2, :].rearrange("p e d -> p (e d)"))
                    mm.then_inc(s["d_mm"], 1)

                def neighbours(t, half):
                    if r is None:
                        return
                    if t == 0 and half == 0:
                        pe.wait_ge(s["b_q"], (r + 1) * 4)
                        pe.wait_ge(s["b_p2"], r + 1)
                    if half == 0 and not (isinstance(r, int) and r * T + t == 0):
                        pe.wait_ge(s["r_n"], r * T + t)
                    for h in range(H // 2 * half, H // 2 * (half + 1)):
                        at = h % (H // 2) * 2 * X1
                        for u in range(T):
                            for i in range(PARTS):
                                pe.matmul(bR[:, half, at:at + 2 * X1], below[:, par, u, h, t * P:(t + 1) * P],
                                          xp[:, par, u, i, h * 2 * X1:(h + 1) * 2 * X1],
                                          start=at + u + i == 0, stop=False, skip_group_check=True)
                    for u in range(T):
                        for i in range(PARTS):
                            mm = pe.matmul(bR[:, half, 0:H * X1].rearrange("p (h c) -> p h c", c=2 * X1)[:, :, 0:X1],
                                           mtn[:, par, u, t * P:(t + 1) * P],
                                           xp[:, par, u, i, half * H * X1:(half + 1) * H * X1].rearrange("p (h c) -> p h c", c=2 * X1)[:, :, 0:X1],
                                           start=False, stop=u == T - 1 and i == PARTS - 1, skip_group_check=True)
                    if half == 1:
                        mm.then_inc(s["r_mm"], 1)

                def projection(t):
                    three(bX[:, 0:D + HA], lambda k: xTh[:, k, t, :], lambda k: xTl[:, k, t, :],
                          lambda k: Wph[:, k, :], lambda k: Wpl[:, k, :]).then_inc(s["a_xp"], 1)

                def turn(to, g, rows, ready, done):
                    pe.wait_ge(s[ready], (g + 1) * T)
                    for k in range(K):
                        for t in range(T):
                            mm = pe.transpose(to[:, (k * T + t) * P:(k * T + t + 1) * P], rows[:, t, k * P:(k + 1) * P], ident[:, :])
                    mm.then_inc(s[done], 1)

                def mask_turned():
                    pe.wait_ge(s["a_mb"], a + 1)
                    pe.wait_ge(s["a_row"], a + 1)
                    for u in range(T):
                        for t in range(T):
                            mm = pe.transpose(bS[:, 0:N].bitcast(BF16)[:, (u * T + t) * P:(u * T + t + 1) * P], mb[:, t, u, :], ident16[:, :])
                    mm.then_inc(s["a_mT"], 1)

                def logits():
                    if not (isinstance(c, int) and c == 0):
                        pe.wait_ge(s["c_cTs"], c)
                    else:
                        pe.wait_ge(s["a_mneg"], a)
                    if isinstance(c, int) and c == 0:
                        pe.wait_ge(s["gate_lo"], 1)
                    pe.wait_ge(s["c_lo"], c + 1)
                    for k in range(K):
                        for i, p in enumerate((fTh, fTl)):
                            mm = pe.matmul(bS[0:2 * E, 0:N], gate2[:, k, :], p[:, other, k].rearrange("p t n -> p (t n)"),
                                           start=k == 0 and i == 0, stop=k == K - 1 and i == 1)
                    mm.then_inc(s["c_lT"], 1)

                def source_rows():
                    if isinstance(a, int) and a == 0:
                        pe.wait_ge(s["mod_sb"], 3)
                    pe.wait_ge(s["a_src"], a + 1)
                    if c is not None:
                        held(pe, "c_lg", c + 1)
                    elif a:
                        pe.wait_ge(s["a_mneg"], a)
                    for t in range(T):
                        mm = pe.transpose(bS[0:H, t * P:(t + 1) * P], asrc2[:, par, t, :], ident[:, :])
                    mm.then_inc(s["a_rT"], 1)

                def node_mean():
                    if a is not None:
                        pe.wait_ge(s["a_ev"], (a + 1) * T)
                    pe.wait_ge(s["b_sum"], b + 1)
                    pe.matmul(bX[:, 0:D].rearrange("p (h k) -> p h k", h=H), mean_w[:, :], xsum[:, :, :],
                              start=True, stop=True).then_inc(s["b_S"], 1)

                neighbours(0, 0)
                chunk(0)
                neighbours(0, 1)
                if a is not None:
                    if c is not None and not (isinstance(c, int) and c == 0):
                        pe.wait_ge(s["c_lo"], c)
                    turn(bT, a, xn, "a_xn", "a_xT")
                chunk(1)
                chunk(2)
                if a is not None:
                    pe.wait_ge(s["a_lo"], a + 1)
                    if not (isinstance(a, int) and a <= 1):
                        pe.wait_ge(s["b_Sb"], a - 1)
                    projection(0)
                if c is not None:
                    turn(bT, c, xf, "c_xn", "c_xT")
                chunk(3)
                if a is not None:
                    pe.wait_ge(s["a_ev"], a * T + 1)
                    projection(1)
                neighbours(1, 0)
                if c is not None:
                    logits()
                chunk(4)
                if c is not None:
                    held(pe, "c_lTs", c + 1)
                    for t in range(T):
                        mm = pe.transpose(bS[:, 2 * t * E:2 * (t + 1) * E], lgT[:, t * P:(t + 1) * P], ident[0:2 * E, 0:2 * E])
                    mm.then_inc(s["c_lb"], 1)
                neighbours(1, 1)
                if a is not None:
                    source_rows()
                if b is not None:
                    node_mean()
                chunk(5)
                if a is not None:
                    mask_turned()
                chunk(6)
                chunk(7)
                if c is not None:
                    if a is not None:
                        held(pe, "a_mneg", a + 1)
                    held(pe, "c_c3", c + 1)
                    for t in range(T):
                        mm = pe.transpose(bS[0:3 * E, t * P:(t + 1) * P], c3[:, t].rearrange("p a b -> p (a b)"), ident[:, :])
                    mm.then_inc(s["c_cT"], 1)
                chunk(8)
                if isinstance(a, int) and a < FILL:
                    v_rows(a)

            with pe.If(fast_path(pe) == 1):
                iterations(pe, body)
            with pe.Else():
                pe.wait_ge(s["mod_sb"], 3)
                for piece in range(FILL):
                    v_rows(piece)
                pe.wait_ge(s["v_sb"], 1)
                with pe.Fori(0, G) as g:
                    pe.wait_ge(s["xn_d"], (g + 1) * T)
                    for k in range(K):
                        for t in range(T):
                            mm = pe.transpose(pT[:, (k * T + t) * P:(k * T + t + 1) * P], xn[:, t, k * P:(k + 1) * P], ident[:, :])
                    mm.then_inc(s["xT_mm"], 1)
                    pe.wait_ge(s["xTl_d"], g + 1)
                    for t, bk in enumerate((pA, pB)):
                        for k in range(K):
                            for i, (a, b) in enumerate(((xTh, Wph), (xTh, Wpl), (xTl, Wph))):
                                mm = pe.matmul(bk[:, 0:D + HA], a[:, k, t, :], b[:, k, :], start=k == 0 and i == 0, stop=k == K - 1 and i == 2)
                    mm.then_inc(s["xp_mm"], 1)
                    pe.wait_ge(s["adst_d"], (g + 1) * T)
                    pe.wait_ge(s["xh_d"], (g + 1) * T)
                    for n in range(T * H):
                        t, h = n // H, n % H
                        i = g * T * H + n + 1
                        if n:
                            pe.wait_ge(s["vmax_d"], i - 1)
                        for u in range(T):
                            mm = pe.transpose(pC[:, u * P:(u + 1) * P], adst[:, u, h:h + 1].broadcast_to([P, P]), ident[:, :])
                        mm.then_inc(s["bc_mm"], 1)
                        pe.wait_ge(s["prob_d"], i)
                        for u in range(T):
                            mm = pe.transpose(pT[:, u * P:(u + 1) * P], prob[:, u * P:(u + 1) * P], ident[:, :])
                        mm.then_inc(s["pT_mm"], 1)
                        pe.wait_ge(s["pT_d"], i)
                        if n:
                            pe.wait_ge(s["att_d"], i - 1)
                        for u in range(T):
                            mm = pe.matmul(pA[:, 0:KH], probT[:, u, :], xh[:, u, h * KH:(h + 1) * KH], start=u == 0, stop=u == T - 1)
                        mm.then_inc(s["o_mm"], 1)
                with pe.Fori(0, G) as g:
                    pe.wait_ge(s["fxn_d"], (g + 1) * T)
                    for k in range(K):
                        for t in range(T):
                            mm = pe.transpose(pT[:, (k * T + t) * P:(k * T + t + 1) * P], xn[:, t, k * P:(k + 1) * P], ident[:, :])
                    mm.then_inc(s["fxT_mm"], 1)
                    pe.wait_ge(s["fxTl_d"], g + 1)
                    for t in range(T):
                        for k in range(K):
                            for i, (a, b) in enumerate(((xTh, gateh), (xTh, gatel), (xTl, gateh))):
                                mm = pe.matmul(pA[:, t * E:(t + 1) * E], a[:, k, t, :], b[:, k, :], start=k == 0 and i == 0, stop=k == K - 1 and i == 2)
                    mm.then_inc(s["lg_mm"], 1)
                    pe.wait_ge(s["cmb_d"], (g + 1) * T)
                    for t in range(T):
                        mm = pe.transpose(pB[0:E, t * P:(t + 1) * P], cmb[:, t, :], ident[:, :])
                    mm.then_inc(s["cT_mm"], 1)
                    pe.wait_ge(s["cT_d"], g + 1)
                    for t in range(T):
                        mm = pe.matmul(pC[:, t * D:(t + 1) * D], cT[:, t, :], V[:, :], start=True, stop=True)
                    mm.then_inc(s["v_mm"], 1)
                    for b in range(T * E // 2):
                        q, t = b // T, b % T
                        if b >= 4:
                            pe.wait_ge(s["e_acc"], g * T * E + 2 * (b - 3))
                        for k in range(K):
                            for i, (a, w) in enumerate(((xTh, Weh), (xTh, Wel), (xTl, Weh))):
                                mm = pe.matmul(pE[b % 4][:, :], a[:, k, t, :], w[:, k, 2 * q:2 * q + 2, :].rearrange("p e d -> p (e d)"),
                                               start=k == 0 and i == 0, stop=k == K - 1 and i == 2)
                        mm.then_inc(s["e_mm"], 1)


_INS = ["x", "adj", "L0_gnn_W_proj", "L0_gnn_W_att", "L0_gnn_b_att", "L0_ffn_Ins_tk", "L0_ffn_gate_w",
        "L0_ffn_expert_w", "L0_ffn_expert_b", "L0_ffn_gamma_w", "L0_ffn_beta_w", "L0_ffn_rmod_w"]


def kernel(**inputs):
    import concourse.bacc as bacc
    import numpy as np
    from concourse.bass_utils import run_bass_kernel_spmd

    nc = bacc.Bacc("TRN2", target_bir_lowering=False, num_devices=1)
    arrays, args = {}, []
    for name in _INS:
        a = np.asarray(inputs[name])
        a = np.ascontiguousarray(a.T if name == "L0_ffn_gamma_w" else a)
        arrays[f"in_{name}"] = a
        args.append(nc.dram_tensor(f"in_{name}", a.shape, mybir.dt.from_np(a.dtype), kind="ExternalInput").ap())
    out = nc.dram_tensor("out", arrays["in_x"].shape, F32, kind="ExternalOutput").ap()
    program(nc, *args, out)
    result = run_bass_kernel_spmd(nc, [arrays], core_ids=[0])
    return result.results[0]["out"]
```
